# Optimizing a Trainium2 kernel written in Bass

```python
import numpy as np
import jax
import jax.numpy as jnp

def _softmax(x, axis=-1):
    return jax.nn.softmax(x, axis=axis)

def _gelu(x):
    return jax.nn.gelu(x, approximate=True)

def _silu(x):
    return jax.nn.silu(x)

def _sigmoid(x):
    return jax.nn.sigmoid(x)

def _layernorm(x, axis=-1, eps=1e-05):
    m = jnp.mean(x, axis=axis, keepdims=True)
    v = jnp.var(x, axis=axis, keepdims=True)
    return (x - m) / jnp.sqrt(v + eps)

def _scatter_add(tgt, idx, src, axis=0):
    return tgt.at[idx].add(src)

def _segment_sum(src, seg, n):
    return jax.ops.segment_sum(src, seg, n)
kernel_name = 'mk_seq_preln_d1_jaxref_r8_8e9254'

def setup_inputs(seed: int=0):
    np.random.seed(seed)
    _w = jnp.asarray

    def _L0_attn_setup():
        import jax, jax.numpy as jnp
        import numpy as np
        B, T, HID = (1, 256, 256)
        H = 16
        D = HID // H
        EPS = 1e-05

        def _layer_norm(x, eps=1e-05):
            mu = jnp.mean(x, axis=-1, keepdims=True)
            var = jnp.mean((x - mu) ** 2, axis=-1, keepdims=True)
            return (x - mu) * jax.lax.rsqrt(var + eps)

        def _feature_map(x, gamma, beta):
            return _layer_norm(x * gamma + beta)
        key = jax.random.key(seed)
        ks = jax.random.split(key, 8)
        s = HID ** (-0.5)
        return {'hidden_states': jax.random.normal(ks[0], (B, T, HID), jnp.float32), 'Wq': jax.random.normal(ks[1], (HID, HID), jnp.float32) * s, 'Wk': jax.random.normal(ks[2], (HID, HID), jnp.float32) * s, 'Wv': jax.random.normal(ks[3], (HID, HID), jnp.float32) * s, 'Wo': jax.random.normal(ks[4], (HID, HID), jnp.float32) * s, 'gamma': 1.0 + 0.1 * jax.random.normal(ks[5], (D,), jnp.float32), 'beta': 0.1 * jax.random.normal(ks[6], (D,), jnp.float32)}
    _L0_attn_in = _L0_attn_setup()

    def _L0_ffn_setup():
        import jax, jax.numpy as jnp
        import numpy as np
        E = 64
        K = 6
        CAP = 64
        SCALE = 1.0
        H = 256
        I = 96
        SI = I * 2
        B, S = (2, 128)

        def _moe(x, gate_w, gate_up_proj, down_proj, shared_gate_w, shared_up_w, shared_down_w):
            b, s, h = x.shape
            T = b * s
            xf = x.reshape(T, h)
            scores = jax.nn.softmax(xf @ gate_w.T, axis=-1)
            topk_w, topk_idx = jax.lax.top_k(scores, K)
            topk_w = topk_w * SCALE
            flat_e = topk_idx.reshape(-1)
            order = jnp.argsort(flat_e)
            sorted_e = flat_e[order]
            sorted_tok = (order // K).astype(jnp.int32)
            sorted_w = topk_w.reshape(-1)[order]
            counts = jnp.zeros((E,), jnp.int32).at[flat_e].add(1)
            offsets = jnp.cumsum(counts) - counts
            pos = jnp.arange(T * K, dtype=jnp.int32) - offsets[sorted_e]
            buf_tok = jnp.full((E, CAP), T, jnp.int32).at[sorted_e, pos].set(sorted_tok, mode='drop')
            buf_w = jnp.zeros((E, CAP), x.dtype).at[sorted_e, pos].set(sorted_w, mode='drop')
            xp = jnp.concatenate([xf, jnp.zeros((1, h), x.dtype)], axis=0)
            gx = xp[buf_tok]
            gu = jnp.einsum('ech,ehi->eci', gx, gate_up_proj)
            g, u = jnp.split(gu, 2, axis=-1)
            hid = jax.nn.silu(g) * u
            eo = jnp.einsum('eci,eih->ech', hid, down_proj) * buf_w[..., None]
            routed = jnp.zeros((T + 1, h), x.dtype).at[buf_tok.reshape(-1)].add(eo.reshape(-1, h))[:T]
            shared = jax.nn.silu(xf @ shared_gate_w.T) * (xf @ shared_up_w.T) @ shared_down_w.T
            return (routed + shared).reshape(b, s, h)
        key = jax.random.key(seed)
        ks = jax.random.split(key, 7)
        x = jax.random.normal(ks[0], (B, S, H), jnp.float32)
        gate_w = jax.random.normal(ks[1], (E, H), jnp.float32) * 0.02
        gate_up_proj = jax.random.normal(ks[2], (E, H, 2 * I), jnp.float32) * 0.02
        down_proj = jax.random.normal(ks[3], (E, I, H), jnp.float32) * 0.02
        shared_gate_w = jax.random.normal(ks[4], (SI, H), jnp.float32) * 0.02
        shared_up_w = jax.random.normal(ks[5], (SI, H), jnp.float32) * 0.02
        shared_down_w = jax.random.normal(ks[6], (H, SI), jnp.float32) * 0.02
        return dict(x=x, gate_w=gate_w, gate_up_proj=gate_up_proj, down_proj=down_proj, shared_gate_w=shared_gate_w, shared_up_w=shared_up_w, shared_down_w=shared_down_w)
    _L0_ffn_in = _L0_ffn_setup()
    _d = {'L0_attn_hidden_states': _L0_attn_in['hidden_states'], 'L0_attn_Wq': _L0_attn_in['Wq'], 'L0_attn_Wk': _L0_attn_in['Wk'], 'L0_attn_Wv': _L0_attn_in['Wv'], 'L0_attn_Wo': _L0_attn_in['Wo'], 'L0_attn_gamma': _L0_attn_in['gamma'], 'L0_attn_beta': _L0_attn_in['beta'], 'L0_ffn_gate_w': _L0_ffn_in['gate_w'], 'L0_ffn_gate_up_proj': _L0_ffn_in['gate_up_proj'], 'L0_ffn_down_proj': _L0_ffn_in['down_proj'], 'L0_ffn_shared_gate_w': _L0_ffn_in['shared_gate_w'], 'L0_ffn_shared_up_w': _L0_ffn_in['shared_up_w'], 'L0_ffn_shared_down_w': _L0_ffn_in['shared_down_w']}
    _x0 = _d['L0_attn_hidden_states']
    _d['L0_attn_hidden_states'] = jax.random.normal(jax.random.fold_in(jax.random.key(seed), 1), (16, 256, 256), dtype=_x0.dtype)
    del _x0
    return _d

def reference(L0_attn_hidden_states, L0_attn_Wq, L0_attn_Wk, L0_attn_Wv, L0_attn_Wo, L0_attn_gamma, L0_attn_beta, L0_ffn_gate_w, L0_ffn_gate_up_proj, L0_ffn_down_proj, L0_ffn_shared_gate_w, L0_ffn_shared_up_w, L0_ffn_shared_down_w):

    def _L0_attn_ref(hidden_states, Wq, Wk, Wv, Wo, gamma, beta):
        import jax, jax.numpy as jnp
        import numpy as np
        B, T, HID = (1, 256, 256)
        H = 16
        D = HID // H
        EPS = 1e-05

        def _layer_norm(x, eps=1e-05):
            mu = jnp.mean(x, axis=-1, keepdims=True)
            var = jnp.mean((x - mu) ** 2, axis=-1, keepdims=True)
            return (x - mu) * jax.lax.rsqrt(var + eps)

        def _feature_map(x, gamma, beta):
            return _layer_norm(x * gamma + beta)
        b, t, _ = hidden_states.shape
        q = (hidden_states @ Wq.T).reshape(b, t, H, D)
        k = (hidden_states @ Wk.T).reshape(b, t, H, D)
        v = (hidden_states @ Wv.T).reshape(b, t, H, D)
        q = _feature_map(q, gamma, beta)
        k = _feature_map(k, gamma, beta)
        q = q * D ** (-0.5)
        attn = jnp.einsum('bqhd,bkhd->bhqk', q, k) ** 2
        mask = jnp.tril(jnp.ones((t, t), dtype=bool))
        attn = jnp.where(mask, attn, 0.0)
        o = jnp.einsum('bhqk,bkhd->bqhd', attn, v)
        z = jnp.sum(attn, axis=-1)
        o = o / (jnp.swapaxes(z, 1, 2)[..., None] + EPS)
        o = o.reshape(b, t, H * D)
        return o @ Wo.T

    def _L0_ffn_ref(x, gate_w, gate_up_proj, down_proj, shared_gate_w, shared_up_w, shared_down_w):
        import jax, jax.numpy as jnp
        import numpy as np
        E = 64
        K = 6
        CAP = 64
        SCALE = 1.0
        H = 256
        I = 96
        SI = I * 2
        B, S = (2, 128)

        def _moe(x, gate_w, gate_up_proj, down_proj, shared_gate_w, shared_up_w, shared_down_w):
            b, s, h = x.shape
            T = b * s
            xf = x.reshape(T, h)
            scores = jax.nn.softmax(xf @ gate_w.T, axis=-1)
            topk_w, topk_idx = jax.lax.top_k(scores, K)
            topk_w = topk_w * SCALE
            flat_e = topk_idx.reshape(-1)
            order = jnp.argsort(flat_e)
            sorted_e = flat_e[order]
            sorted_tok = (order // K).astype(jnp.int32)
            sorted_w = topk_w.reshape(-1)[order]
            counts = jnp.zeros((E,), jnp.int32).at[flat_e].add(1)
            offsets = jnp.cumsum(counts) - counts
            pos = jnp.arange(T * K, dtype=jnp.int32) - offsets[sorted_e]
            buf_tok = jnp.full((E, CAP), T, jnp.int32).at[sorted_e, pos].set(sorted_tok, mode='drop')
            buf_w = jnp.zeros((E, CAP), x.dtype).at[sorted_e, pos].set(sorted_w, mode='drop')
            xp = jnp.concatenate([xf, jnp.zeros((1, h), x.dtype)], axis=0)
            gx = xp[buf_tok]
            gu = jnp.einsum('ech,ehi->eci', gx, gate_up_proj)
            g, u = jnp.split(gu, 2, axis=-1)
            hid = jax.nn.silu(g) * u
            eo = jnp.einsum('eci,eih->ech', hid, down_proj) * buf_w[..., None]
            routed = jnp.zeros((T + 1, h), x.dtype).at[buf_tok.reshape(-1)].add(eo.reshape(-1, h))[:T]
            shared = jax.nn.silu(xf @ shared_gate_w.T) * (xf @ shared_up_w.T) @ shared_down_w.T
            return (routed + shared).reshape(b, s, h)
        return _moe(x, gate_w, gate_up_proj, down_proj, shared_gate_w, shared_up_w, shared_down_w)
    x = L0_attn_hidden_states
    x = x + _L0_attn_ref(_layernorm(x, axis=-1), L0_attn_Wq, L0_attn_Wk, L0_attn_Wv, L0_attn_Wo, L0_attn_gamma, L0_attn_beta)
    x = x + _L0_ffn_ref(_layernorm(x, axis=-1), L0_ffn_gate_w, L0_ffn_gate_up_proj, L0_ffn_down_proj, L0_ffn_shared_gate_w, L0_ffn_shared_up_w, L0_ffn_shared_down_w)
    return x

_drawn_inputs = setup_inputs


def setup_inputs(seed=0):
    import zlib

    import numpy as np

    out = dict(_drawn_inputs(seed))
    spreads = {}
    factors = {'L0_ffn_gate_w': 8.0,
     'L0_ffn_gate_up_proj': 8.0,
     'L0_ffn_down_proj': 8.0,
     'L0_ffn_shared_gate_w': 4.003,
     'L0_ffn_shared_up_w': 3.932,
     'L0_ffn_shared_down_w': 3.952}
    for name, (base, spread) in spreads.items():
        noise = np.random.default_rng([zlib.crc32(name.encode()), seed]).standard_normal(out[name].shape)
        drawn = base * np.exp(spread * noise) if base else spread * noise
        out[name] = jnp.asarray(drawn.astype(out[name].dtype))
    for name, factor in factors.items():
        out[name] = (out[name] * factor).astype(out[name].dtype)
    return out
```

```python
from contextlib import ExitStack

import numpy as np
import concourse.bass as bass
from concourse import mybir

F32, F16, BF16 = mybir.dt.float32, mybir.dt.float16, mybir.dt.bfloat16
I32, U32 = mybir.dt.int32, mybir.dt.uint32
ALU = mybir.AluOpType
ACT = mybir.ActivationFunctionType
AX = mybir.AxisListType.X

P = 128
NB, T, H = 16, 256, 256
NT = NB * T
HEADS, D = 16, 16
E, K, CAP = 64, 6, 64
I2 = 96
EPS = 1e-5
PAIRS = E // 2
ROW = H + E
ROWS = NT + P
U = 8

C_ID, C_BLK, C_TRI, C_ONE = 0, 128, 160, 288
C_DIAG, C_IOTA, C_P1, C_DUMP, C_HALF = 416, 432, 440, 441, 449
C_N = 453


def constants():
    c = np.zeros((P, C_N), np.float32)
    p = np.arange(P)
    c[:, C_ID:C_ID + P] = np.eye(P)
    for i in range(8):
        c[16 * i:16 * i + 16, C_BLK + i] = 1.0 / D
    c[:, C_TRI:C_TRI + P] = p[:, None] < p[None, :]
    c[:, C_ONE:C_ONE + P] = 1.0
    c[:, C_DIAG:C_DIAG + 16] = (p[:, None] // 8) == np.arange(16)
    c[:, C_IOTA:C_IOTA + 8] = np.arange(8)
    c[:, C_P1] = p + 1
    c[:, C_DUMP:C_DUMP + 8] = NT + 1 + (p[:, None] % 16) * 8 + np.arange(8)
    low = p < 64
    c[:, C_HALF] = low
    c[:, C_HALF + 1] = np.where(low, 0, NT + p)
    c[:, C_HALF + 2] = ~low
    c[:, C_HALF + 3] = np.where(low, NT + p, 0)
    return c


class Step:

    def __init__(self, n, parity):
        self.n, self.parity = n, parity

    def batch(self, offset):
        return self.n + offset, (self.parity + offset) % 2


def need(eng, sem, count):
    if isinstance(count, int) and count <= 0:
        return
    eng.wait_ge(sem, count)


def plain_wait(eng, ready, *counts):
    counts = [c for c in counts if not isinstance(c, int)]
    if counts:
        for c in counts:
            eng.to_reg(c)
        eng.wait_ge(ready, 1)


def block_kernel(nc, x, wq, wk, wv, wo, gamma, beta, wg, wgu, wdn, wsg, wsu, wsd, const, out):
    with ExitStack() as ctx:
        def sb(name, shape, dt=F32):
            return ctx.enter_context(nc.sbuf_tensor(name, shape, dt))

        sems = {}

        def sem(name):
            if name not in sems:
                sems[name] = ctx.enter_context(nc.semaphore(name))
            return sems[name]

        def dram(name, shape, dt=F32):
            return nc.dram_tensor(name, shape, dt, kind="Internal").ap()

        q_stack_d = [dram(f"q_stack_d{i}", (HEADS * 4 * D, T), F16) for i in range(2)]
        k_stack_d = [dram(f"k_stack_d{i}", (HEADS * 4 * D, T), F16) for i in range(2)]
        rows_d = dram("rows_d", (ROWS, ROW))
        acc_d = [dram(f"acc_d{i}", (ROWS, H)) for i in range(2)]
        table_d = dram("table_d", (E * CAP,))

        bank = [ctx.enter_context(nc.psum_tensor(f"bank{i}", [P, 512], F32)) for i in range(8)]
        S_BANK, O_BANK, G_BANK = bank[0:4], bank[4], bank[5:8]

        cst = sb("cst", [P, C_N])
        ident = cst[:, C_ID:C_ID + P]
        blk = cst[:, C_BLK:C_BLK + 32]
        tri_b = sb("tri_b", [P, P], BF16)
        one_b = sb("one_b", [P, P], BF16)
        x_all = sb("x_all", [P, 2 * NB, H])
        w_raw = sb("w_raw", [P, 2, 768])
        w_tmp = sb("w_tmp", [P, 2, 512])
        w_mean = sb("w_mean", [P, 2, 32])
        gb = sb("gb", [P, 2, D])
        b_mean = sb("b_mean", [P, 1])
        b_c = sb("b_c", [P, D])
        b_hi = sb("b_hi", [P, D], F16)
        b_lo = sb("b_lo", [P, D], F16)
        bias_w = sb("bias_w", [P, 8, D], F16)
        frac_b = sb("frac_b", [P, T], F16)
        w_hi = sb("w_hi", [P, 2, 768], F16)
        w_lo = sb("w_lo", [P, 2, 768], F16)
        wo_s = sb("wo_s", [P, 2, H])
        s_raw = sb("s_raw", [P, 2, 448])
        s_hi = sb("s_hi", [P, 2, 448], F16)
        s_lo = sb("s_lo", [P, 2, 448], F16)
        wsd_s = sb("wsd_s", [I2, 2, H])
        st1 = sb("st1", [P, 2, 6])
        mv1 = sb("mv1", [P, 2, 2])
        ve1 = sb("ve1", [P, 2])
        rs1 = sb("rs1", [P, 2])
        mhalf = sb("mhalf", [P, 2])
        xn = [sb(f"xn{i}", [P, 2, H]) for i in range(2)]
        x_hi = sb("x_hi", [P, 2, T], F16)
        x_lo = sb("x_lo", [P, 2, T], F16)
        q_hl = [sb(f"q_hl{i}", [P, 2, 2, T], F16) for i in range(2)]
        k_hl = [sb(f"k_hl{i}", [P, 2, 2, T], F16) for i in range(2)]
        q_sq = sb("q_sq", [P, 2, T])
        k_sq = sb("k_sq", [P, 2, T])
        var_t = sb("var_t", [P, T])
        k_var = sb("k_var", [P, 2, HEADS])
        k_rec = sb("k_rec", [P, 2, HEADS])
        q_eps = [sb(f"q_eps{i}", [P, 2, HEADS]) for i in range(2)]
        v_w = [sb(f"v_w{i}", [P, 2, HEADS, 32]) for i in range(2)]
        q_st = [sb(f"q_st{i}", [P, 8, T], F16) for i in range(2)]
        k_st = [sb(f"k_st{i}", [P, 8, T], F16) for i in range(2)]
        a_sq = sb("a_sq", [P, 8, 384])
        o_t = sb("o_t", [P, 4, T])
        den = sb("den", [P, 2, HEADS])
        rec = sb("rec", [P, 2, HEADS])
        o_n = sb("o_n", [P, 2, H])
        o_nt = sb("o_nt", [P, 2, T])
        st2 = sb("st2", [P, 2, 6])
        mv2 = sb("mv2", [P, 2, 2])
        ve2 = sb("ve2", [P, 2])
        rs2 = sb("rs2", [P, 2])
        row = [sb(f"row{i}", [P, 2, ROW]) for i in range(2)]
        x2_hi = sb("x2_hi", [P, 2, T], F16)
        x2_lo = sb("x2_lo", [P, 2, T], F16)
        th = sb("th", [I2, 2 * T])
        t1 = sb("t1", [I2, 2 * T])
        hs = sb("hs", [I2, 2, T])
        y = [sb(f"y{i}", [P, 2, H]) for i in range(2)]
        gmax = sb("gmax", [P, 2])
        gneg = sb("gneg", [P, 2])
        gsum = sb("gsum", [P, 2])
        grec = sb("grec", [P, 2])
        ex = sb("ex", [P, 2, 72])
        top = sb("top", [P, 2, 8])
        top6 = sb("top6", [P, 2, 8])
        marked = sb("marked", [P, 2, 72])
        chosen = [sb(f"chosen{i}", [P, 2, E], BF16) for i in range(2)]
        before = [sb(f"before{i}", [P, E], BF16) for i in range(2)]
        both = sb("both", [P, E], BF16)
        pos_f = sb("pos_f", [P, 2 * E])
        pos_i = sb("pos_i", [P, 2 * E], I32)
        pos_lo = sb("pos_lo", [P, 2 * E], I32)
        pos_hi = sb("pos_hi", [P, 2 * E], I32)
        tile_no = sb("tile_no", [P, 2])
        hi_hot = sb("hi_hot", [P, 2, E, 8], BF16)
        lo_hot = sb("lo_hot", [P, 2, E, 8], BF16)
        tok_hot = sb("tok_hot", [P, 2, E, 2, 8], BF16)
        table = sb("table", [P, 4, 16, 16])
        tab_s = sb("tab_s", [P, 4, 16])
        tab_t = sb("tab_t", [P, 4, 8])
        tab_e = sb("tab_e", [P, 4, 8])
        tab_u = sb("tab_u", [P, 4, 8])
        tab_r = sb("tab_r", [PAIRS, P])
        slot_tok = sb("slot_tok", [P, PAIRS], U32)
        slot_a = sb("slot_a", [P, PAIRS], U32)
        slot_b = sb("slot_b", [P, PAIRS], U32)
        idx_g = sb("idx_g", [P, U], U32)
        idx_a = sb("idx_a", [P, U], U32)
        idx_b = sb("idx_b", [P, U], U32)
        zero = sb("zero", [P, ROW])
        w_gu = [sb(f"w_gu{i}", [P, 2, 2, 2 * I2]) for i in range(U)]
        w_dn = [sb(f"w_dn{i}", [I2, 2, H]) for i in range(U)]
        spare = a_sq[:].rearrange("p s m -> p (s m)")
        g_x = [spare[:, ROW * i:ROW * i + ROW] for i in range(4)]
        g_xt = [spare[:, 4 * ROW + H * i:4 * ROW + H * i + H].rearrange("p (c s) -> p c s", c=2) for i in range(2)]
        e_o = [spare[:, 4 * ROW + 2 * H + H * i:4 * ROW + 3 * H + H * i] for i in range(4)]
        e_th = [sb(f"e_th{i}", [P, I2]) for i in range(2)]
        e_t1 = [sb(f"e_t1{i}", [P, I2]) for i in range(2)]
        e_h = [sb(f"e_h{i}", [P, I2]) for i in range(2)]
        e_ht = [sb(f"e_ht{i}", [I2, P]) for i in range(2)]
        f_a = [x_all[:, 4 * i:4 * i + 4, :] for i in range(2)]
        f_b = [x_all[:, 8 + 4 * i:12 + 4 * i, :] for i in range(2)]

        x_d = x.rearrange("b (t p) h -> b p t h", p=P)
        out_d = out.rearrange("b (t p) h -> (b t) p h", p=P)
        rows_t = rows_d[0:NT, :].rearrange("(b t p) h -> b p t h", t=2, p=P)
        acc0_t = acc_d[0][0:NT, :].rearrange("(b t p) h -> b p t h", t=2, p=P)

        def pairs_of_blocks(ap):
            return ap.rearrange("p (s d) -> p s d", d=D)

        USES = ["xtr", "pos", "otr0", "otr1", "q", "k", "ontr", "var", "wo", "vtr", "v",
                "x2tr", "sg", "su", "gate", "so", "cmp0", "cmp1"]
        STAGE = {"xtr": 1, "q": 1, "k": 1, "var": 1, "vtr": 1, "v": 1, "otr0": -1, "otr1": -1, "ontr": -1,
                 "wo": -1, "x2tr": -2, "sg": -2, "su": -2, "gate": -2, "so": -2, "pos": -3, "cmp0": -3, "cmp1": -3}

        def g_bank(use):
            return G_BANK[USES.index(use) % 3]

        def active(s, offset):
            return not isinstance(s.n, int) or 0 <= s.n + offset < NB

        def bank_free(pe, s, use):
            i = USES.index(use)
            for back in range(1, 7):
                j = i - 3 * back
                prev, steps = USES[j % 18], (0 if j >= 0 else 1)
                b = s.n - steps + STAGE[prev]
                if isinstance(b, int) and not 0 <= b < NB:
                    continue
                pe.wait_ge(sem(prev + "_read"), b + 1)
                return

        block = ctx.enter_context(nc.Block())

        def pipeline(eng, body, first=-2):
            for n in range(first, 4):
                body(Step(n, n % 2))
            with eng.Fori(2, 6) as i:
                body(Step(2 * i, 0))
                body(Step(2 * i + 1, 1))
            for n in range(12, NB + 3):
                body(Step(n, n % 2))

        def load_expert(sp, pair, u):
            sp.dma_start(w_gu[u][:], wgu[bass.ds(2 * pair, 2)].rearrange("e (c p) m -> p e c m", p=P)).then_inc(sem(f"w_expert{u}"), 16)
            sp.dma_start(w_dn[u][:], wdn[bass.ds(2 * pair, 2)].rearrange("e p h -> p e h")).then_inc(sem(f"w_expert{u}"), 16)

        def load_sum(sp, j, u):
            for a, f in ((0, f_a), (1, f_b)):
                src = acc_d[a][0:NT, :].rearrange("(j t p) h -> j p t h", t=4, p=P)
                sp.dma_start(f[u], src[bass.ds(j, 1)].rearrange("o p t h -> p (o t) h")).then_inc(sem(f"sum_in{u}"), 16)

        def store_sum(sp, j, u):
            dst = out.rearrange("b (t p) h -> (b t) p h", p=P).rearrange("(j t) p h -> j p t h", t=4)
            sp.dma_start(dst[bass.ds(j, 1)].rearrange("o p t h -> p (o t) h"), f_a[u]).then_inc(sem("sum_out"), 16)

        @block.sync
        def _(sp):
            sp.dma_start(cst[:], const).then_inc(sem("const_in"), 16)
            sp.dma_start(gb[:, 0, :], gamma.rearrange("(o d) -> o d", o=1).to_broadcast([P, D])).then_inc(sem("w_in"), 16)
            sp.dma_start(gb[:, 1, :], beta.rearrange("(o d) -> o d", o=1).to_broadcast([P, D])).then_inc(sem("w_in"), 16)
            for i, w in enumerate((wq, wk, wv)):
                sp.dma_start(w_raw[:, :, 256 * i:256 * i + 256],
                             w.rearrange("(c p) m -> p c m", p=P)).then_inc(sem("w_in"), 16)
            for b in range(2):
                sp.dma_start(x_all[:, 2 * b:2 * b + 2, :], x_d[b]).then_inc(sem(f"x_in{b}"), 16)
            sp.dma_start(x_all[:, 4:6, :], x_d[2]).then_inc(sem("x_in"), 16)
            sp.dma_start(wo_s[:], wo.rearrange("(c p) m -> p c m", p=P)).then_inc(sem("w_in"), 16)
            for i, (w, m) in enumerate(((wsg, 192), (wsu, 192), (wg, 64))):
                sp.dma_start(s_raw[:, :, 192 * i:192 * i + m],
                             w.rearrange("(c p) m -> p c m", p=P)).then_inc(sem("w_in"), 16)
            sp.dma_start(wsd_s[:], wsd.rearrange("(m p) h -> p m h", p=I2)).then_inc(sem("w_in"), 16)
            sp.wait_ge(sem("zeroed"), 1)
            sp.dma_start(rows_d[NT:ROWS, :], zero[:]).then_inc(sem("zero_out"), 16)
            sp.dma_start(acc_d[0][NT:ROWS, :], zero[:, 0:H]).then_inc(sem("zero_out"), 16)
            for i in range(ROWS // P):
                sp.dma_start(acc_d[1][i * P:(i + 1) * P, :], zero[:, 0:H]).then_inc(sem("zero_out"), 16)
            for i in range(U):
                load_expert(sp, i, i)

            def body(s):
                if active(s, 3) and not (isinstance(s.n, int) and s.n < 0):
                    b, _p = s.batch(3)
                    sp.wait_ge(sem("x_in"), 16 * (s.n + 1))
                    sp.dma_start(x_all[:, bass.ds(2 * b, 2), :],
                                 x_d[bass.ds(b, 1)].rearrange("o p t h -> p (o t) h")).then_inc(sem("x_in"), 16)
                if active(s, -3):
                    b, p = s.batch(-3)
                    sp.wait_ge(sem("so_read"), b + 1)
                    sp.dma_start(acc0_t[bass.ds(b, 1)].rearrange("o p t h -> p (o t) h"), y[p][:]).then_inc(sem("y_out"), 16)
                    sp.wait_ge(sem("row"), b + 1)
                    sp.dma_start(rows_t[bass.ds(b, 1)].rearrange("o p t h -> p (o t) h"), row[p][:]).then_inc(sem("row_out"), 16)
                if active(s, 1):
                    b, p = s.batch(1)
                    plain_wait(sp, sem("ready"), 32 * (b - 1))
                    need(sp, sem("stack_in"), 32 * (b - 1))
                    for name, src, dst, order in (("q", q_hl, q_stack_d, (0, 0, 1, 1)), ("k", k_hl, k_stack_d, (0, 1, 0, 1))):
                        sp.wait_ge(sem(name + "_read"), b + 1)
                        for r, part in enumerate(order):
                            for c in range(2):
                                d4 = dst[p].rearrange("(h r d) t -> r h d t", h=HEADS, r=4)
                                sp.dma_start(d4[r, 8 * c:8 * c + 8], src[p][:, part, c, :]).then_inc(sem("stack_out"), 16)
                    sp.wait_ge(sem("stack_out"), 256 * (b + 1))
                    need(sp, sem("score7"), b - 1)
                    sp.dma_start(q_st[p][:], q_stack_d[p].rearrange("(g q) t -> q g t", q=P)).then_inc(sem("stack_in"), 16)
                    sp.dma_start(k_st[p][:], k_stack_d[p].rearrange("(g q) t -> q g t", q=P)).then_inc(sem("stack_in"), 16)

            pipeline(sp, body)

            sp.wait_ge(sem("tab_u"), 1)
            sp.dma_start(table_d.rearrange("(g p b) -> p g b", g=4, p=P), tab_u[:]).then_inc(sem("table_out"), 16)
            sp.wait_ge(sem("table_out"), 16)
            sp.dma_start(tab_r[:], table_d.rearrange("(g p) -> g p", p=P)).then_inc(sem("table_in"), 16)
            with sp.Fori(0, PAIRS // U - 1) as i:
                for u in range(U):
                    plain_wait(sp, sem("ready"), U * i + u + 1)
                    need(sp, sem("e_down"), U * i + u + 1)
                    load_expert(sp, U * i + U + u, u)
            sp.wait_ge(sem("added_a"), 16 * PAIRS)
            sp.wait_ge(sem("added_b"), 16 * PAIRS)
            load_sum(sp, 0, 0)
            load_sum(sp, 1, 1)
            with sp.Fori(0, 3) as i:
                for u in range(2):
                    sp.wait_ge(sem("summed"), 2 * i + u + 1)
                    store_sum(sp, 2 * i + u, u)
                    sp.wait_ge(sem("sum_out"), 16 * (2 * i + u + 1))
                    load_sum(sp, 2 * i + u + 2, u)
            for j in (6, 7):
                sp.wait_ge(sem("summed"), j + 1)
                store_sum(sp, j, j % 2)
            sp.wait_ge(sem("sum_out"), 128)
            sp.wait_ge(sem("zero_out"), 16 * (2 + ROWS // P))

        @block.tensor
        def _(pe):
            def split3(o, w, xx, first, last):
                pe.matmul(o, w[0], xx[0], start=first, stop=False)
                pe.matmul(o, w[1], xx[0], start=False, stop=False)
                return pe.matmul(o, w[0], xx[1], start=False, stop=last)

            def scores(s, g):
                b, p = s.batch(0)
                if g == 0:
                    pe.wait_ge(sem("stack_in"), 32 * (b + 1))
                for h in range(4 * g, 4 * g + 4):
                    if h % 2 == 0:
                        pair = h // 2
                        need(pe, sem(f"square{(pair - 2) % 8}"), b + 1 if pair >= 2 else b)
                    q = 64 * (h % 2)
                    o = S_BANK[h % 4]
                    kk, qq = k_st[p][q:q + 64, h // 2, :], q_st[p][q:q + 64, h // 2, :]
                    pe.matmul(o[:, 0:128], kk[:, 128:256], qq[:, 128:256], start=True, stop=True, tile_position=(q, 0))
                    mm = pe.matmul(o[:, 128:384], kk[:, 0:128], qq, start=True, stop=True, tile_position=(q, 0))
                    if h % 2:
                        mm.then_inc(sem(f"score{h // 2}"), 1)

            def values(s, g):
                b, p = s.batch(0)
                if g == 0:
                    pe.wait_ge(sem("v_read"), b + 1)
                pe.wait_ge(sem(f"masked{g}"), b + 1)
                if g % 2 == 0:
                    need(pe, sem("o_read1") if g == 0 else sem("o_read0"), b if g == 0 else b + 1)
                c = 256 * (g % 2)
                for j in range(4):
                    h = 4 * g + j
                    pe.matmul(O_BANK[32 * j:32 * j + 32, c:c + 256], v_w[p][:, 0, h, :], a_sq[:, h % 8, 128:384],
                              start=True, stop=False, tile_position=(0, 32 * j), skip_group_check=True)
                for j in range(4):
                    h = 4 * g + j
                    mm = pe.matmul(O_BANK[32 * j:32 * j + 32, c + 128:c + 256], v_w[p][:, 1, h, :], a_sq[:, h % 8, 0:128],
                                   start=False, stop=True, tile_position=(0, 32 * j), skip_group_check=True)
                mm.then_inc(sem(f"value{g}"), 1)

            def transposes(s, use, src, after):
                bank_free(pe, s, use)
                pe.wait_ge(*after)
                o = g_bank(use)
                for c in range(2):
                    for t in range(2):
                        tr = pe.transpose(o[:, 256 * c + 128 * t:256 * c + 128 * t + 128], src[:, t, 128 * c:128 * c + 128], ident)
                tr.then_inc(sem(use), 1)

            def project(s, use, first_col):
                b, p = s.batch(1)
                bank_free(pe, s, use)
                pe.wait_ge(sem("xtr_read"), b + 1)
                for m in range(2):
                    o = g_bank(use)[:, 256 * m:256 * m + 256]
                    pe.matmul(o, bias_w[:].rearrange("p i d -> p (i d)"), frac_b[:], start=True, stop=False)
                    for c in range(2):
                        cols = slice(first_col + 128 * m, first_col + 128 * m + 128)
                        mm = split3(o, (w_hi[:, c, cols], w_lo[:, c, cols]), (x_hi[:, c, :], x_lo[:, c, :]), False, c == 1)
                mm.then_inc(sem(use), 1)

            def body(s):
                if active(s, 0):
                    scores(s, 0)
                if active(s, 1):
                    b, p = s.batch(1)
                    transposes(s, "xtr", xn[p], (sem("xn"), b + 1))
                if active(s, -3):
                    b, p = s.batch(-3)
                    bank_free(pe, s, "pos")
                    pe.wait_ge(sem("chosen"), b + 1)
                    pe.wait_ge(sem("before"), b + 1)
                    o = g_bank("pos")
                    pe.matmul(o[:, 0:64], one_b[:], before[p][:], start=True, stop=False)
                    pe.matmul(o[:, 0:64], tri_b[:], chosen[p][:, 0, :], start=False, stop=True)
                    pe.matmul(o[:, 64:128], one_b[:], before[p][:], start=True, stop=False)
                    pe.matmul(o[:, 64:128], one_b[:], chosen[p][:, 0, :], start=False, stop=False)
                    pe.matmul(o[:, 64:128], tri_b[:], chosen[p][:, 1, :], start=False, stop=True).then_inc(sem("pos"), 1)
                if active(s, -1):
                    b, p = s.batch(-1)
                    for t in range(2):
                        bank_free(pe, s, f"otr{t}")
                        pe.wait_ge(sem("o_read1"), b + 1)
                        for g in range(4):
                            tr = pe.transpose(g_bank(f"otr{t}")[:, 128 * g:128 * g + 128], o_t[:, g, 128 * t:128 * t + 128], ident)
                        tr.then_inc(sem(f"otr{t}"), 1)
                if active(s, 0):
                    scores(s, 1)
                if active(s, 1):
                    project(s, "q", 0)
                if active(s, 0):
                    values(s, 0)
                if active(s, 1):
                    project(s, "k", 256)
                if active(s, -1):
                    b, p = s.batch(-1)
                    transposes(s, "ontr", o_n, (sem("otr1_read"), b + 1))
                if active(s, 0):
                    scores(s, 2)
                if active(s, 1):
                    b, p = s.batch(1)
                    bank_free(pe, s, "var")
                    pe.wait_ge(sem("q_sq"), b + 1)
                    pe.wait_ge(sem("k_sq"), b + 1)
                    for j in range(4):
                        mm = pe.matmul(g_bank("var")[32 * j:32 * j + 32, 0:256], blk, (q_sq, k_sq)[j // 2][:, j % 2, :],
                                       start=True, stop=True, tile_position=(0, 32 * j))
                    mm.then_inc(sem("var"), 1)
                if active(s, 0):
                    values(s, 1)
                if active(s, -1):
                    b, p = s.batch(-1)
                    bank_free(pe, s, "wo")
                    pe.wait_ge(sem("ontr_read"), b + 1)
                    for t in range(2):
                        for c in range(2):
                            mm = pe.matmul(g_bank("wo")[:, 256 * t:256 * t + 256], o_nt[:, c, 128 * t:128 * t + 128],
                                           wo_s[:, c, :], start=c == 0, stop=c == 1)
                    mm.then_inc(sem("wo"), 1)
                if active(s, 1):
                    b, p = s.batch(1)
                    bank_free(pe, s, "vtr")
                    pe.wait_ge(sem("var_read"), b + 1)
                    for t in range(2):
                        tr = pe.transpose(g_bank("vtr")[:, 128 * t:128 * t + 128], var_t[:, 128 * t:128 * t + 128], ident)
                    tr.then_inc(sem("vtr"), 1)
                if active(s, 0):
                    scores(s, 3)
                if active(s, 1):
                    b, p = s.batch(1)
                    bank_free(pe, s, "v")
                    for t in range(2):
                        for c in range(2):
                            tok = slice(128 * t, 128 * t + 128)
                            mm = split3(g_bank("v")[:, 256 * t:256 * t + 256], (x_hi[:, c, tok], x_lo[:, c, tok]),
                                        (w_hi[:, c, 512:768], w_lo[:, c, 512:768]), c == 0, c == 1)
                    mm.then_inc(sem("v"), 1)
                if active(s, -2):
                    b, p = s.batch(-2)
                    transposes(s, "x2tr", row[p], (sem("x2n"), b + 1))
                if active(s, 0):
                    values(s, 2)
                if active(s, -2):
                    b, p = s.batch(-2)
                    for use, first in (("sg", 0), ("su", 192)):
                        bank_free(pe, s, use)
                        pe.wait_ge(sem("x2tr_read"), b + 1)
                        for m in range(2):
                            for c in range(2):
                                cols = slice(first + I2 * m, first + I2 * m + I2)
                                mm = split3(g_bank(use)[0:I2, 256 * m:256 * m + 256], (s_hi[:, c, cols], s_lo[:, c, cols]),
                                            (x2_hi[:, c, :], x2_lo[:, c, :]), c == 0, c == 1)
                        mm.then_inc(sem(use), 1)
                    bank_free(pe, s, "gate")
                    for t in range(2):
                        for c in range(2):
                            tok = slice(128 * t, 128 * t + 128)
                            mm = split3(g_bank("gate")[:, 64 * t:64 * t + 64], (x2_hi[:, c, tok], x2_lo[:, c, tok]),
                                        (s_hi[:, c, 384:448], s_lo[:, c, 384:448]), c == 0, c == 1)
                    mm.then_inc(sem("gate"), 1)
                if active(s, 0):
                    values(s, 3)
                if active(s, -2):
                    b, p = s.batch(-2)
                    bank_free(pe, s, "so")
                    pe.wait_ge(sem("su_read"), b + 1)
                    for t in range(2):
                        for m in range(2):
                            mm = pe.matmul(g_bank("so")[:, 256 * t:256 * t + 256], hs[:, m, 128 * t:128 * t + 128],
                                           wsd_s[:, m, :], start=m == 0, stop=m == 1)
                    mm.then_inc(sem("so"), 1)
                if active(s, -3):
                    b, p = s.batch(-3)
                    for half in range(2):
                        use = f"cmp{half}"
                        bank_free(pe, s, use)
                        pe.wait_ge(sem("tok_hot"), b + 1)
                        for gr in range(2):
                            ex16 = slice(32 * half + 16 * gr, 32 * half + 16 * gr + 16)
                            for t in range(2):
                                mm = pe.matmul(g_bank(use)[:, 256 * gr:256 * gr + 256],
                                               hi_hot[:, t, ex16, :].rearrange("p e a -> p (e a)"),
                                               tok_hot[:, t, ex16, :, :].rearrange("p e w b -> p (e w b)"),
                                               start=t == 0, stop=t == 1)
                        mm.then_inc(sem(use), 1)

            pe.wait_ge(sem("const_in"), 16)
            pe.wait_ge(sem("w_ready"), 2)
            pe.wait_ge(sem("w_in"), 16 * 10)
            pipeline(pe, body)

            def gather_t(i, pair, u):
                pe.wait_ge(sem(f"gathered{u % 4}"), 16 * (2 * i + u // 4 + 1))
                need(pe, sem("g_xt"), pair - 1)
                o = bank[u % 2]
                for c in range(2):
                    tr = pe.transpose(o[:, 128 * c:128 * c + 128], g_x[u % 4][:, 128 * c:128 * c + 128], ident)
                tr.then_inc(sem("gtr"), 1)

            def gate_up(i, pair, u):
                pe.wait_ge(sem("g_xt"), pair + 1)
                pe.wait_ge(sem(f"w_expert{u}"), 32 * (i + 1))
                need(pe, sem("e_h"), pair - 1)
                o = bank[2 + u % 2]
                for c in range(2):
                    for e in range(2):
                        mm = pe.matmul(o[64 * e:64 * e + 64, 0:2 * I2], g_xt[u % 2][:, c, 64 * e:64 * e + 64], w_gu[u][:, e, c, :],
                                       start=c == 0, stop=c == 1, tile_position=(0, 64 * e), skip_group_check=True)
                mm.then_inc(sem("gu"), 1)

            def hidden_t(pair, u):
                pe.wait_ge(sem("e_h"), pair + 1)
                need(pe, sem("e_ht"), pair - 1)
                pe.transpose(bank[4 + u % 2][0:I2, 0:P], e_h[u % 2][:], ident).then_inc(sem("htr"), 1)

            def down(i, pair, u):
                pe.wait_ge(sem("e_ht"), pair + 1)
                pe.wait_ge(sem(f"w_expert{u}"), 32 * (i + 1))
                need(pe, sem("e_o"), pair - 1)
                o = bank[6 + u % 2]
                for e in range(2):
                    mm = pe.matmul(o[64 * e:64 * e + 64, 0:H], e_ht[u % 2][:, 64 * e:64 * e + 64], w_dn[u][:, e, :],
                                   start=True, stop=True, tile_position=(0, 64 * e), skip_group_check=True)
                mm.then_inc(sem("e_down"), 1)

            def experts(i):
                for u in range(U):
                    pair = U * i + u
                    gather_t(i, pair, u)
                    gate_up(i, pair, u)
                    hidden_t(pair, u)
                    down(i, pair, u)

            pe.wait_ge(sem("o_read1"), NB)
            pe.wait_ge(sem("cmp0_read"), NB)
            pe.wait_ge(sem("cmp1_read"), NB)
            pe.wait_ge(sem("pos_read"), NB)
            pe.wait_ge(sem("table_in"), 16)
            pe.transpose(bank[0][:, 0:PAIRS], tab_r[:], ident[0:PAIRS, 0:PAIRS]).then_inc(sem("table_t"), 1)
            pe.wait_ge(sem("slots"), 3)
            experts(0)
            with pe.Fori(1, PAIRS // U) as i:
                experts(i)

        @block.scalar
        def _(act):
            def squares(s, pair):
                b, p = s.batch(0)
                act.wait_ge(sem(f"score{pair}"), b + 1)
                need(act, sem(f"value{(pair // 2 - 2) % 4}"), b + 1 if pair >= 4 else b)
                for h in (2 * pair, 2 * pair + 1):
                    sq = act.activation(a_sq[:, h % 8, :], S_BANK[h % 4][:, 0:384], ACT.Square)
                sq.then_inc(sem(f"square{pair}"), 1)

            def out_copy(s, half):
                b, p = s.batch(0)
                act.wait_ge(sem(f"value{2 * half + 1}"), b + 1)
                if half == 0:
                    need(act, sem("otr1"), b)
                act.copy(o_t[:, 2 * half:2 * half + 2, :].rearrange("p g t -> p (g t)"), O_BANK[:]).then_inc(sem(f"o_read{half}"), 1)

            def flat(ap):
                return ap.rearrange("p c t -> p (c t)")

            def body(s):
                if active(s, 0):
                    squares(s, 0)
                    squares(s, 1)
                if active(s, 1):
                    b, p = s.batch(1)
                    act.wait_ge(sem("xtr"), b + 1)
                    need(act, sem("v"), b)
                    act.copy(flat(x_hi[:]), g_bank("xtr")[:]).then_inc(sem("x_hi"), 1)
                if active(s, 0):
                    squares(s, 2)
                    squares(s, 3)
                if active(s, 1):
                    b, p = s.batch(1)
                    for use, hl, sq in (("q", q_hl, q_sq), ("k", k_hl, k_sq)):
                        act.wait_ge(sem(use), b + 1)
                        if use == "q":
                            need(act, sem("stack_out"), 256 * (b - 1))
                            need(act, sem("var"), b)
                        act.copy(hl[p][:, 0, :, :].rearrange("p c t -> p (c t)"), g_bank(use)[:]).then_inc(sem(use + "_hi"), 1)
                        act.activation(flat(sq[:]), g_bank(use)[:], ACT.Square).then_inc(sem(use + "_sq"), 1)
                if active(s, -1):
                    b, p = s.batch(-1)
                    act.wait_ge(sem("ontr"), b + 1)
                    need(act, sem("wo"), b)
                    act.copy(flat(o_nt[:]), g_bank("ontr")[:]).then_inc(sem("ontr_read"), 1)
                if active(s, 0):
                    squares(s, 4)
                    squares(s, 5)
                    out_copy(s, 0)
                if active(s, 1):
                    b, p = s.batch(1)
                    act.wait_ge(sem("var"), b + 1)
                    need(act, sem("vtr"), b)
                    act.copy(var_t[:], g_bank("var")[:, 0:256]).then_inc(sem("var_read"), 1)
                if active(s, 0):
                    squares(s, 6)
                    squares(s, 7)
                if active(s, -2):
                    b, p = s.batch(-2)
                    act.wait_ge(sem("x2tr"), b + 1)
                    need(act, sem("gate"), b)
                    act.copy(flat(x2_hi[:]), g_bank("x2tr")[:]).then_inc(sem("x2_hi"), 1)
                    act.wait_ge(sem("sg"), b + 1)
                    need(act, sem("sg_read"), b)
                    act.activation(th[:], g_bank("sg")[0:I2, :], ACT.Tanh, scale=0.5).then_inc(sem("th"), 1)
                    act.wait_ge(sem("gneg"), b + 1)
                    need(act, sem("chosen"), b)
                    need(act, sem("row"), b)
                    for t in range(2):
                        e = act.activation(ex[:, t, 0:64], g_bank("gate")[:, 64 * t:64 * t + 64], ACT.Exp,
                                           bias=gneg[:, t:t + 1], accum_out=gsum[:, t:t + 1])
                    e.then_inc(sem("gate_read"), 1)
                if active(s, 0):
                    out_copy(s, 1)

            act.wait_ge(sem("ready"), 1)
            pipeline(act, body)

            def experts(i):
                for u in range(U):
                    pair = U * i + u
                    act.wait_ge(sem("gtr"), pair + 1)
                    need(act, sem("gu"), pair - 1)
                    act.copy(g_xt[u % 2].rearrange("p c s -> p (c s)"), bank[u % 2][:, 0:256]).then_inc(sem("g_xt"), 1)
                    act.wait_ge(sem("gu"), pair + 1)
                    need(act, sem("e_t1"), pair - 1)
                    act.activation(e_th[u % 2][:], bank[2 + u % 2][:, 0:I2], ACT.Tanh, scale=0.5).then_inc(sem("e_th"), 1)
                    act.wait_ge(sem("htr"), pair + 1)
                    need(act, sem("e_down"), pair - 1)
                    act.copy(e_ht[u % 2][:], bank[4 + u % 2][0:I2, 0:P]).then_inc(sem("e_ht"), 1)

            experts(0)
            with act.Fori(1, PAIRS // U) as i:
                experts(i)

        @block.gpsimd
        def _(pool):
            pool.memset(zero[:], 0.0).then_inc(sem("zeroed"), 1)

            def masks(s, pair):
                b, p = s.batch(0)
                plain_wait(pool, sem("ready"), b + 1)
                need(pool, sem(f"square{pair}"), b + 1)
                h = 2 * pair % 8
                a = a_sq[:, h:h + 2, 0:2 * P]
                m = pool.affine_select(out=a, in_=a, pattern=[[0, 2], [0, 2], [1, P]], compare_op=ALU.is_ge, fill=0.0,
                                       base=0, channel_multiplier=-1)
                if pair % 2:
                    m.then_inc(sem(f"masked{pair // 2}"), 1)

            def body(s):
                if active(s, 2):
                    b, p = s.batch(2)
                    pool.wait_ge(sem("ve1"), b + 1)
                    need(pool, sem("xn"), b)
                    pool.tensor_tensor(rs1[:], ve1[:], mhalf[:], ALU.pow).then_inc(sem("rs1"), 1)
                if active(s, 0):
                    for pair in range(6):
                        masks(s, pair)
                if active(s, -1):
                    b, p = s.batch(-1)
                    pool.wait_ge(sem("ve2"), b + 1)
                    need(pool, sem("x2n"), b)
                    pool.tensor_tensor(rs2[:], ve2[:], mhalf[:], ALU.pow).then_inc(sem("rs2"), 1)
                if active(s, 0):
                    for pair in range(6, 8):
                        masks(s, pair)

            pool.wait_ge(sem("ready"), 1)
            pipeline(pool, body)

            pool.wait_ge(sem("slots"), 3)
            pool.wait_ge(sem("row_out"), 16 * NB)
            pool.wait_ge(sem("y_out"), 16 * NB)
            pool.wait_ge(sem("zero_out"), 16 * (2 + ROWS // P))

            def gather(pair, u, col):
                plain_wait(pool, sem("ready"), pair - 3)
                need(pool, sem("e_h"), pair - 3)
                need(pool, sem("gtr"), pair - 3)
                pool.indirect_dma_start(out=g_x[u % 4], out_offset=None, in_=rows_d[:, :],
                                        in_offset=bass.IndirectOffsetOnAxis(ap=col, axis=0)).then_inc(sem(f"gathered{u % 4}"), 16)

            def scatter(pair, u):
                plain_wait(pool, sem("ready"), pair + 1, 16 * pair)
                pool.wait_ge(sem("e_o"), pair + 1)
                for name, idx, dst in (("added_a", idx_a, acc_d[0]), ("added_b", idx_b, acc_d[1])):
                    plain_wait(pool, sem("ready"), 16 * pair)
                    need(pool, sem(name), 16 * pair)
                    pool.indirect_dma_start(out=dst[:, :], out_offset=bass.IndirectOffsetOnAxis(ap=idx[:, u:u + 1], axis=0),
                                            in_=e_o[u % 4], in_offset=None, compute_op=ALU.add).then_inc(sem(name), 16)

            def experts(i):
                if not isinstance(i, int):
                    pool.wait_ge(sem("added_a"), 16 * U * i)
                    pool.wait_ge(sem("added_b"), 16 * U * i)
                for j, (dst, src) in enumerate(((idx_g, slot_tok), (idx_a, slot_a), (idx_b, slot_b))):
                    pool.tensor_copy(dst[:], src[:, bass.ds(U * i, U)]).then_inc(sem("idx"), 1)
                pool.wait_ge(sem("idx"), 3 * i + 3)
                for u in range(3):
                    gather(U * i + u, u, idx_g[:, u:u + 1])
                for u in range(U):
                    if u + 3 < U:
                        gather(U * i + u + 3, u + 3, idx_g[:, u + 3:u + 4])
                    scatter(U * i + u, u)

            experts(0)
            with pool.Fori(1, PAIRS // U) as i:
                experts(i)

        @block.vector
        def _(dve):
            done = [0]

            def chain(ins):
                done[0] += 1
                ins.then_inc(sem("setup"), 1)
                dve.wait_ge(sem("setup"), done[0])

            for i in range(2):
                chain(dve.memset(v_w[i][:].rearrange("p t h c -> p (t h c)"), 0.0))
            chain(dve.memset(mhalf[:], -0.5))
            chain(dve.memset(frac_b[:], 1.0 / 64))
            chain(dve.memset(ex[:].rearrange("p t e -> p (t e)"), -2.0))
            chain(dve.memset(top6[:].rearrange("p t e -> p (t e)"), -2.0))
            chain(dve.memset(before[0][:], 0.0))
            chain(dve.memset(table[:].rearrange("p g e w -> p (g e w)"), 0.0))
            chain(dve.memset(tile_no[:, 0:1], -2.0))
            chain(dve.memset(tile_no[:, 1:2], -1.0))
            dve.wait_ge(sem("const_in"), 16)
            chain(dve.tensor_copy(tri_b[:], cst[:, C_TRI:C_TRI + P]))
            chain(dve.tensor_copy(one_b[:], cst[:, C_ONE:C_ONE + P]))
            chain(dve.memset(b_mean[:], 0.0))
            dve.memset(b_c[:], 0.0).then_inc(sem("ready"), 1)
            dve.wait_ge(sem("ready"), 1)

            def ln1(b, p, x_pair):
                for t in range(2):
                    st = dve.bn_stats(st1[:, t, :], x_pair[:, t, :])
                st.then_inc(sem("st1"), 1)
                plain_wait(dve, sem("ready"), b + 1)
                need(dve, sem("st1"), b + 1)
                for t in range(2):
                    ag = dve.bn_aggr(mv1[:, t, :], st1[:, t, :])
                ag.then_inc(sem("mv1"), 1)
                dve.wait_ge(sem("mv1"), b + 1)
                need(dve, sem("rs1"), b)
                dve.tensor_scalar(ve1[:], mv1[:, :, 1], EPS, None, ALU.add).then_inc(sem("ve1"), 1)

            def ln1_apply(b, p, x_pair):
                dve.wait_ge(sem("rs1"), b + 1)
                need(dve, sem("xtr"), b - 1)
                for t in range(2):
                    n = dve.tensor_scalar(xn[p][:, t, :], x_pair[:, t, :], mv1[:, t, 0:1], rs1[:, t:t + 1], ALU.subtract, ALU.mult)
                n.then_inc(sem("xn"), 1)

            def flat(ap):
                return ap.rearrange("p c t -> p (c t)")

            def positions(s):
                b, p = s.batch(-3)
                need(dve, sem("tok_hot"), b)
                dve.tensor_scalar(tile_no[:], tile_no[:], 2.0, None, ALU.add).then_inc(sem("tile_no"), 1)
                ch = chosen[p][:].rearrange("p t e -> p (t e)")
                dve.wait_ge(sem("pos"), b + 1)
                dve.scalar_tensor_tensor(pos_f[:], ch, -1024.0, g_bank("pos")[:, 0:128], ALU.mult, ALU.add).then_inc(sem("pos_read"), 1)
                dve.tensor_tensor(both[:], chosen[p][:, 0, :], chosen[p][:, 1, :], ALU.add).then_inc(sem("both"), 1)
                dve.wait_ge(sem("both"), b + 1)
                dve.tensor_tensor(before[1 - p][:], before[p][:], both[:], ALU.add).then_inc(sem("before"), 1)
                dve.wait_ge(sem("pos_read"), b + 1)
                dve.tensor_scalar(pos_i[:], pos_f[:], 1024.0, None, ALU.add).then_inc(sem("pos_i"), 1)

            def one_hots(s):
                b, p = s.batch(-3)
                dve.wait_ge(sem("pos_i"), b + 1)
                dve.tensor_scalar(pos_lo[:], pos_i[:], 7, None, ALU.bitwise_and)
                dve.tensor_scalar(pos_hi[:], pos_i[:], 3, None, ALU.arith_shift_right).then_inc(sem("digits"), 1)
                dve.wait_ge(sem("digits"), b + 1)
                need(dve, sem("cmp1"), b)
                digits = cst[:, C_IOTA:C_IOTA + 8].unsqueeze(1).to_broadcast([P, 2 * E, 8])
                for dst, src in ((hi_hot, pos_hi), (lo_hot, pos_lo)):
                    hot = dve.tensor_tensor(dst[:].rearrange("p t e d -> p (t e) d"), src[:].unsqueeze(2).to_broadcast([P, 2 * E, 8]),
                                            digits, ALU.is_equal)
                hot.then_inc(sem("lo_hot"), 1)
                dve.wait_ge(sem("lo_hot"), b + 1)
                dve.wait_ge(sem("tile_no"), b + 1)
                dve.tensor_scalar(tok_hot[:, :, :, 0, :].rearrange("p t e d -> p (t e) d"),
                                  lo_hot[:].rearrange("p t e d -> p (t e) d"), cst[:, C_P1:C_P1 + 1], None, ALU.mult)
                for t in range(2):
                    th_ = dve.tensor_scalar(tok_hot[:, t, :, 1, :], lo_hot[:, t, :, :], tile_no[:, t:t + 1], None, ALU.mult)
                th_.then_inc(sem("tok_hot"), 1)

            def low_part(b, use, hi_sem, hi, lo, after_sem):
                dve.wait_ge(sem(hi_sem), b + 1)
                dve.tensor_tensor(lo, g_bank(use)[:], hi, ALU.subtract).then_inc(sem(after_sem), 1)

            def body(s):
                x_of = lambda b: x_all[:, bass.ds(2 * b, 2), :] if not isinstance(b, int) else x_all[:, 2 * b:2 * b + 2, :]
                if active(s, 2):
                    b, p = s.batch(2)
                    if isinstance(b, int) and b < 2:
                        dve.wait_ge(sem(f"x_in{b}"), 16)
                    else:
                        plain_wait(dve, sem("ready"), 16 * (b - 1))
                        dve.wait_ge(sem("x_in"), 16 * (b - 1))
                    ln1(b, p, x_of(b))
                if active(s, 1):
                    b, p = s.batch(1)
                    dve.wait_ge(sem("x_hi"), b + 1)
                    need(dve, sem("v"), b)
                    dve.tensor_tensor(flat(x_lo[:]), g_bank("xtr")[:], flat(x_hi[:]), ALU.subtract).then_inc(sem("xtr_read"), 1)
                if active(s, -3):
                    positions(s)
                if active(s, -1):
                    b, p = s.batch(-1)
                    for t in range(2):
                        dve.wait_ge(sem(f"otr{t}"), b + 1)
                        o = g_bank(f"otr{t}")[:].rearrange("p (h c) -> p h c", c=32)
                        dd = dve.tensor_tensor(den[:, t, :], o[:, :, 16], q_eps[p][:, t, :], ALU.add)
                    dd.then_inc(sem("den"), 1)
                    dve.wait_ge(sem("den"), b + 1)
                    dve.reciprocal(rec[:].rearrange("p t h -> p (t h)"), den[:].rearrange("p t h -> p (t h)")).then_inc(sem("rec"), 1)
                    dve.wait_ge(sem("rec"), b + 1)
                    need(dve, sem("ontr"), b)
                    for t in range(2):
                        o = g_bank(f"otr{t}")[:].rearrange("p (h c) -> p h c", c=32)
                        r = rec[:, t, :].unsqueeze(2).to_broadcast([P, HEADS, D])
                        on = dve.tensor_tensor(o_n[:, t, :].rearrange("p (h d) -> p h d", d=D), o[:, :, 0:16], r, ALU.mult)
                        on.then_inc(sem(f"otr{t}_read"), 1)
                if active(s, 2):
                    b, p = s.batch(2)
                    ln1_apply(b, p, x_of(b))
                if active(s, 1):
                    b, p = s.batch(1)
                    for use, hl in (("q", q_hl), ("k", k_hl)):
                        dve.wait_ge(sem(use + "_hi"), b + 1)
                        dve.wait_ge(sem(use + "_sq"), b + 1)
                        dve.tensor_tensor(flat(hl[p][:, 1, :, :]), g_bank(use)[:], flat(hl[p][:, 0, :, :]),
                                          ALU.subtract).then_inc(sem(use + "_read"), 1)
                if active(s, -3):
                    one_hots(s)
                if active(s, -1):
                    b, p = s.batch(-1)
                    dve.wait_ge(sem("wo"), b + 1)
                    xx = x_of(b)
                    dve.tensor_tensor(xx, xx, g_bank("wo")[:].rearrange("p (t h) -> p t h", t=2), ALU.add).then_inc(sem("wo_read"), 1)
                    plain_wait(dve, sem("ready"), b + 1)
                    need(dve, sem("wo_read"), b + 1)
                    for t in range(2):
                        st = dve.bn_stats(st2[:, t, :], xx[:, t, :])
                    st.then_inc(sem("st2"), 1)
                    plain_wait(dve, sem("ready"), b + 1)
                    need(dve, sem("st2"), b + 1)
                    for t in range(2):
                        ag = dve.bn_aggr(mv2[:, t, :], st2[:, t, :])
                    ag.then_inc(sem("mv2"), 1)
                    dve.wait_ge(sem("mv2"), b + 1)
                    dve.tensor_scalar(ve2[:], mv2[:, :, 1], EPS, None, ALU.add).then_inc(sem("ve2"), 1)
                if active(s, 1):
                    b, p = s.batch(1)
                    dve.wait_ge(sem("vtr"), b + 1)
                    g = g_bank("vtr")[:, 0:256].rearrange("p (t w m i) -> p t w m i", t=2, w=2, m=2)
                    as4 = lambda a: a.rearrange("p t (m i) -> p t m i", m=2)
                    for t in range(2):
                        gv = g[:, t, 1, :, 0:8]
                        kv = k_var[:, t, :].rearrange("p (m i) -> p m i", m=2)
                        dve.tensor_scalar(kv, gv, EPS, None, ALU.add)
                        gq = g[:, t, 0, :, 0:8]
                        qe = q_eps[p][:, t, :].rearrange("p (m i) -> p m i", m=2)
                        vr = dve.tensor_scalar(qe, gq, EPS, 16 * EPS, ALU.add, ALU.mult)
                    vr.then_inc(sem("vtr_read"), 1)
                    dve.wait_ge(sem("vtr_read"), b + 1)
                    dve.reciprocal(k_rec[:].rearrange("p t h -> p (t h)"), k_var[:].rearrange("p t h -> p (t h)")).then_inc(sem("k_rec"), 1)
                    dve.wait_ge(sem("k_rec"), b + 1)
                    need(dve, sem("value3"), b - 1)
                    for t in range(2):
                        dve.tensor_copy(v_w[p][:, t, :, 16], k_rec[:, t, :])
                    dve.wait_ge(sem("v"), b + 1)
                    for t in range(2):
                        r = k_rec[:, t, :].unsqueeze(2).to_broadcast([P, HEADS, D])
                        vv = dve.tensor_tensor(v_w[p][:, t, :, 0:16], g_bank("v")[:, 256 * t:256 * t + 256].rearrange("p (h d) -> p h d", d=D), r, ALU.mult)
                    vv.then_inc(sem("v_read"), 1)
                if active(s, -1):
                    b, p = s.batch(-1)
                    dve.wait_ge(sem("rs2"), b + 1)
                    need(dve, sem("row_out"), 16 * (b - 1))
                    xx = x_of(b)
                    for t in range(2):
                        n = dve.tensor_scalar(row[p][:, t, 0:H], xx[:, t, :], mv2[:, t, 0:1], rs2[:, t:t + 1], ALU.subtract, ALU.mult)
                    n.then_inc(sem("x2n"), 1)
                if active(s, -2):
                    b, p = s.batch(-2)
                    dve.wait_ge(sem("x2_hi"), b + 1)
                    dve.tensor_tensor(flat(x2_lo[:]), g_bank("x2tr")[:], flat(x2_hi[:]), ALU.subtract).then_inc(sem("x2tr_read"), 1)
                    dve.wait_ge(sem("th"), b + 1)
                    dve.scalar_tensor_tensor(t1[:], th[:], 1.0, g_bank("sg")[0:I2, :], ALU.add, ALU.mult).then_inc(sem("sg_read"), 1)
                    dve.wait_ge(sem("sg_read"), b + 1)
                    dve.wait_ge(sem("su"), b + 1)
                    need(dve, sem("so"), b)
                    dve.scalar_tensor_tensor(flat(hs[:]), t1[:], 0.5, g_bank("su")[0:I2, :], ALU.mult, ALU.mult).then_inc(sem("su_read"), 1)
                    dve.wait_ge(sem("gate"), b + 1)
                    dve.tensor_reduce(gmax[:], g_bank("gate")[:, 0:128].rearrange("p (t e) -> p t e", t=2), AX, ALU.max).then_inc(sem("gmax"), 1)
                    dve.wait_ge(sem("gmax"), b + 1)
                    dve.tensor_scalar(gneg[:], gmax[:], -1.0, None, ALU.mult).then_inc(sem("gneg"), 1)
                    dve.wait_ge(sem("gate_read"), b + 1)
                    dve.reciprocal(grec[:], gsum[:]).then_inc(sem("grec"), 1)
                    for t in range(2):
                        mx = dve.max(top[:, t, :], ex[:, t, 0:64])
                    mx.then_inc(sem("top"), 1)
                    dve.wait_ge(sem("grec"), b + 1)
                    for t in range(2):
                        gw = dve.tensor_scalar(row[p][:, t, H:ROW], ex[:, t, 0:64], grec[:, t:t + 1], 0.5, ALU.mult, ALU.mult)
                    gw.then_inc(sem("row"), 1)
                    dve.wait_ge(sem("top"), b + 1)
                    dve.tensor_copy(top6[:, :, 0:6], top[:, :, 0:6]).then_inc(sem("top6"), 1)
                    plain_wait(dve, sem("ready"), b + 1)
                    need(dve, sem("top6"), b + 1)
                    for t in range(2):
                        mr = dve.match_replace(marked[:, t, 0:66], top6[:, t, :], ex[:, t, 0:66], -1.0)
                    mr.then_inc(sem("marked"), 1)
                    dve.wait_ge(sem("marked"), b + 1)
                    need(dve, sem("pos"), b - 1)
                    dve.tensor_scalar(chosen[p][:], marked[:, :, 0:64], 0.0, None, ALU.is_lt).then_inc(sem("chosen"), 1)
                    dve.wait_ge(sem("so"), b + 1)
                    need(dve, sem("y_out"), 16 * (b - 1))
                    dve.tensor_tensor(y[p][:], x_of(b), g_bank("so")[:].rearrange("p (t h) -> p t h", t=2), ALU.add).then_inc(sem("so_read"), 1)
                if active(s, -3):
                    b, p = s.batch(-3)
                    for half in range(2):
                        dve.wait_ge(sem(f"cmp{half}"), b + 1)
                        tb = table[:, 2 * half:2 * half + 2, :, :].rearrange("p g e w -> p (g e w)")
                        dve.tensor_tensor(tb, tb, g_bank(f"cmp{half}")[:], ALU.add).then_inc(sem(f"cmp{half}_read"), 1)

            body(Step(-2, 0))
            dve.wait_ge(sem("w_in"), 16 * 10)
            for c in range(2):
                wt = w_tmp[:, c, :].rearrange("p (h d) -> p h d", d=D)
                chain(dve.tensor_tensor(wt, w_raw[:, c, 0:512].rearrange("p (h d) -> p h d", d=D),
                                        gb[:, 0:1, :].to_broadcast([P, 32, D]), ALU.mult))
                chain(dve.tensor_reduce(w_mean[:, c, :], wt, AX, ALU.add))
                chain(dve.tensor_scalar(w_mean[:, c, :], w_mean[:, c, :], 1.0 / D, None, ALU.mult))
                wm = w_mean[:, c, :].unsqueeze(2).to_broadcast([P, 32, D])
                chain(dve.tensor_tensor(w_raw[:, c, 0:512].rearrange("p (h d) -> p h d", d=D), wt, wm, ALU.subtract))
            chain(dve.tensor_reduce(b_mean[:], gb[:, 1, :], AX, ALU.add))
            chain(dve.tensor_scalar(b_mean[:], b_mean[:], 1.0 / D, None, ALU.mult))
            chain(dve.tensor_scalar(b_c[:], gb[:, 1, :], b_mean[:, 0:1], None, ALU.subtract))
            chain(dve.tensor_copy(b_hi[:], b_c[:]))
            chain(dve.tensor_tensor(b_lo[:], b_c[:], b_hi[:], ALU.subtract))
            for half, src in enumerate((b_hi, b_lo)):
                q = slice(64 * half, 64 * half + 64)
                chain(dve.tensor_copy(bias_w[q, :, :], src[q, :].unsqueeze(1).to_broadcast([64, 8, D])))
            for hi, lo, raw in ((w_hi, w_lo, w_raw), (s_hi, s_lo, s_raw)):
                fl = lambda a: a[:].rearrange("p c m -> p (c m)")
                chain(dve.tensor_copy(fl(hi), fl(raw)))
                dve.tensor_tensor(fl(lo), fl(raw), fl(hi), ALU.subtract).then_inc(sem("w_ready"), 1)
            dve.wait_ge(sem("w_ready"), 2)
            dve.memset(both[:], 0.0).then_inc(sem("before"), 1)
            pipeline(dve, body, -1)

            dve.wait_ge(sem("cmp1_read"), NB)
            diag = cst[:, C_DIAG:C_DIAG + 16].unsqueeze(1).unsqueeze(3).to_broadcast([P, 4, 16, 16])
            chain(dve.tensor_tensor(table[:], table[:], diag, ALU.mult))
            chain(dve.tensor_reduce(tab_s[:], table[:].rearrange("p g e w -> p g w e"), AX, ALU.add))
            place, tile = tab_s[:, :, 0:8], tab_s[:, :, 8:16]
            chain(dve.scalar_tensor_tensor(tab_t[:], tile, float(P), place, ALU.mult, ALU.add))
            dump = cst[:, C_DUMP:C_DUMP + 8].unsqueeze(1).to_broadcast([P, 4, 8])
            chain(dve.scalar_tensor_tensor(tab_e[:], place, 0.0, dump, ALU.is_equal, ALU.mult))
            chain(dve.tensor_tensor(tab_t[:], tab_t[:], tab_e[:], ALU.add))
            dve.tensor_scalar(tab_u[:], tab_t[:], -1.0, None, ALU.add).then_inc(sem("tab_u"), 1)
            dve.wait_ge(sem("table_t"), 1)
            dve.tensor_copy(slot_tok[:], bank[0][:, 0:PAIRS]).then_inc(sem("slots"), 1)
            for i, dst in enumerate((slot_a, slot_b)):
                dve.tensor_scalar(dst[:], bank[0][:, 0:PAIRS], cst[:, C_HALF + 2 * i:C_HALF + 2 * i + 1],
                                  cst[:, C_HALF + 2 * i + 1:C_HALF + 2 * i + 2], ALU.mult, ALU.add).then_inc(sem("slots"), 1)

            def experts(i):
                for u in range(U):
                    pair = U * i + u
                    dve.wait_ge(sem("e_th"), pair + 1)
                    gu = bank[2 + u % 2]
                    dve.scalar_tensor_tensor(e_t1[u % 2][:], e_th[u % 2][:], 1.0, gu[:, 0:I2], ALU.add, ALU.mult).then_inc(sem("e_t1"), 1)
                    dve.wait_ge(sem("e_t1"), pair + 1)
                    need(dve, sem("htr"), pair - 1)
                    dve.wait_ge(sem(f"gathered{u % 4}"), 16 * (2 * i + u // 4 + 1))
                    for e in range(2):
                        q = slice(64 * e, 64 * e + 64)
                        w = g_x[u % 4][q, bass.ds(H + 2 * U * i + 2 * u + e, 1)]
                        eh = dve.scalar_tensor_tensor(e_h[u % 2][q, :], e_t1[u % 2][q, :], w, gu[q, I2:2 * I2], ALU.mult, ALU.mult)
                    eh.then_inc(sem("e_h"), 1)
                    dve.wait_ge(sem("e_down"), pair + 1)
                    need(dve, sem("added_a"), 16 * (pair - 3))
                    need(dve, sem("added_b"), 16 * (pair - 3))
                    dve.tensor_copy(e_o[u % 4], bank[6 + u % 2][:, 0:H]).then_inc(sem("e_o"), 1)

            experts(0)
            with dve.Fori(1, PAIRS // U) as i:
                experts(i)

            def add(j, jj, u):
                dve.wait_ge(sem(f"sum_in{u}"), 32 * (jj + 1))
                fl = lambda a: a.rearrange("p t h -> p (t h)")
                dve.tensor_tensor(fl(f_a[u]), fl(f_a[u]), fl(f_b[u]), ALU.add).then_inc(sem("summed"), 1)

            with dve.Fori(0, 4) as i:
                for u in range(2):
                    add(2 * i + u, i, u)


IN_NAMES = ("x", "wq", "wk", "wv", "wo", "gamma", "beta", "wg", "wgu", "wdn", "wsg", "wsu", "wsd", "const")


def kernel(L0_attn_hidden_states, L0_attn_Wq, L0_attn_Wk, L0_attn_Wv, L0_attn_Wo, L0_attn_gamma, L0_attn_beta,
           L0_ffn_gate_w, L0_ffn_gate_up_proj, L0_ffn_down_proj, L0_ffn_shared_gate_w, L0_ffn_shared_up_w,
           L0_ffn_shared_down_w):
    import numpy as _np
    import concourse.bacc as _bacc
    from concourse import mybir as _mybir
    from concourse.bass_utils import run_bass_kernel_spmd as _run

    laid = (L0_attn_hidden_states, L0_attn_Wq.T, L0_attn_Wk.T, L0_attn_Wv.T, L0_attn_Wo.T, L0_attn_gamma, L0_attn_beta,
            L0_ffn_gate_w.T, L0_ffn_gate_up_proj, L0_ffn_down_proj, L0_ffn_shared_gate_w.T, L0_ffn_shared_up_w.T,
            L0_ffn_shared_down_w.T, constants())
    nc = _bacc.Bacc("TRN2", target_bir_lowering=False, num_devices=1)
    arrays, args = {}, []
    for name, a in zip(IN_NAMES, laid):
        a = _np.ascontiguousarray(a)
        arrays[f"in_{name}"] = a
        args.append(nc.dram_tensor(f"in_{name}", a.shape, _mybir.dt.from_np(a.dtype), kind="ExternalInput").ap())
    out = nc.dram_tensor("out_x", (NB, T, H), _mybir.dt.from_np(_np.dtype("float32")), kind="ExternalOutput").ap()
    block_kernel(nc, *args, out)
    got = _run(nc, [arrays], core_ids=[0])
    return got.results[0]["out_x"]
```

```python
from contextlib import ExitStack

import numpy as np
import concourse.bass as bass
from concourse import mybir

F32, F16, BF16 = mybir.dt.float32, mybir.dt.float16, mybir.dt.bfloat16
I32, U32 = mybir.dt.int32, mybir.dt.uint32
ALU = mybir.AluOpType
ACT = mybir.ActivationFunctionType
AX = mybir.AxisListType.X

P = 128
NB, T, H = 16, 256, 256
NT = NB * T
HEADS, D = 16, 16
E, K, CAP = 64, 6, 64
I2 = 96
EPS = 1e-5
PAIRS = E // 2
ROW = H + E
ROWS = NT + P
U = 8

C_ID, C_BLK, C_TRI, C_ONE = 0, 128, 160, 288
C_DIAG, C_IOTA, C_P1, C_DUMP, C_HALF = 416, 432, 440, 441, 449
C_N = 451


def constants():
    c = np.zeros((P, C_N), np.float32)
    p = np.arange(P)
    c[:, C_ID:C_ID + P] = np.eye(P)
    for i in range(8):
        c[16 * i:16 * i + 16, C_BLK + i] = 1.0 / D
    c[:, C_TRI:C_TRI + P] = p[:, None] < p[None, :]
    c[:, C_ONE:C_ONE + P] = 1.0
    c[:, C_DIAG:C_DIAG + 16] = (p[:, None] // 8) == np.arange(16)
    c[:, C_IOTA:C_IOTA + 8] = np.arange(8)
    c[:, C_P1] = p + 1
    c[:, C_DUMP:C_DUMP + 8] = NT + 1 + (p[:, None] % 16) * 8 + np.arange(8)
    low = p < 64
    c[:, C_HALF] = low
    c[:, C_HALF + 1] = ~low
    return c


class Step:

    def __init__(self, n, parity):
        self.n, self.parity = n, parity

    def batch(self, offset):
        return self.n + offset, (self.parity + offset) % 2


def need(eng, sem, count):
    if isinstance(count, int) and count <= 0:
        return
    eng.wait_ge(sem, count)


def plain_wait(eng, ready, *counts):
    counts = [c for c in counts if not isinstance(c, int)]
    if counts:
        for c in counts:
            eng.to_reg(c)
        eng.wait_ge(ready, 1)


def block_kernel(nc, x, wq, wk, wv, wo, gamma, beta, wg, wgu, wdn, wsg, wsu, wsd, const, out):
    with ExitStack() as ctx:
        def sb(name, shape, dt=F32):
            return ctx.enter_context(nc.sbuf_tensor(name, shape, dt))

        sems = {}

        def sem(name):
            if name not in sems:
                sems[name] = ctx.enter_context(nc.semaphore(name))
            return sems[name]

        def dram(name, shape, dt=F32):
            return nc.dram_tensor(name, shape, dt, kind="Internal").ap()

        q_stack_d = [dram(f"q_stack_d{i}", (HEADS, D, 2, T), F16) for i in range(2)]
        k_stack_d = [dram(f"k_stack_d{i}", (HEADS, D, 2, 2, T), F16) for i in range(2)]
        rows_d = dram("rows_d", (ROWS, ROW))
        table_d = dram("table_d", (E * CAP,))

        bank = [ctx.enter_context(nc.psum_tensor(f"bank{i}", [P, 512], F32)) for i in range(8)]
        S_BANK, O_BANK, G_BANK = bank[0:4], bank[4], bank[5:8]

        cst = sb("cst", [P, C_N])
        ident = cst[:, C_ID:C_ID + P]
        blk = cst[:, C_BLK:C_BLK + 32]
        tri_b = sb("tri_b", [P, P], BF16)
        one_b = sb("one_b", [P, P], BF16)
        x_all = sb("x_all", [P, 2 * NB, H])
        w_raw = sb("w_raw", [P, 2, 768])
        w_tmp = sb("w_tmp", [P, 2, 512])
        w_mean = sb("w_mean", [P, 2, 32])
        gb = sb("gb", [P, 2, D])
        b_mean = sb("b_mean", [P, 1])
        b_c = sb("b_c", [P, D])
        b_hi = sb("b_hi", [P, D], F16)
        b_lo = sb("b_lo", [P, D], F16)
        bias_w = sb("bias_w", [P, 8, D], F16)
        frac_b = sb("frac_b", [P, T], F16)
        w_hi = sb("w_hi", [P, 2, 768], F16)
        w_lo = sb("w_lo", [P, 2, 768], F16)
        wo_s = sb("wo_s", [P, 2, H])
        s_raw = sb("s_raw", [P, 2, 448])
        s_hi = sb("s_hi", [P, 2, 448], F16)
        s_lo = sb("s_lo", [P, 2, 448], F16)
        wsd_s = sb("wsd_s", [I2, 2, H])
        st1 = sb("st1", [P, 2, 6])
        mv1 = sb("mv1", [P, 2, 2])
        ve1 = sb("ve1", [P, 2])
        rs1 = sb("rs1", [P, 2])
        mhalf = sb("mhalf", [P, 2])
        xn = [sb(f"xn{i}", [P, 2, H]) for i in range(2)]
        x_hi = sb("x_hi", [P, 2, T], F16)
        x_lo = sb("x_lo", [P, 2, T], F16)
        q_hl = [sb(f"q_hl{i}", [P, 2, 2, T], F16) for i in range(2)]
        k_hl = [sb(f"k_hl{i}", [P, 2, 2, T], F16) for i in range(2)]
        q_sq = sb("q_sq", [P, 2, T])
        k_sq = sb("k_sq", [P, 2, T])
        var_t = sb("var_t", [P, T])
        k_var = sb("k_var", [P, 2, HEADS])
        k_rec = sb("k_rec", [P, 2, HEADS])
        q_eps = [sb(f"q_eps{i}", [P, 2, HEADS]) for i in range(2)]
        v_w = [sb(f"v_w{i}", [P, 2, HEADS, 32]) for i in range(2)]
        q_st = [sb(f"q_st{i}", [P, 8, T], F16) for i in range(2)]
        k_st = [sb(f"k_st{i}", [P, 8, T], F16) for i in range(2)]
        a_sq = sb("a_sq", [P, 8, 384])
        o_t = sb("o_t", [P, 4, T])
        den = sb("den", [P, 2, HEADS])
        rec = sb("rec", [P, 2, HEADS])
        o_n = sb("o_n", [P, 2, H])
        o_nt = sb("o_nt", [P, 2, T])
        st2 = sb("st2", [P, 2, 6])
        mv2 = sb("mv2", [P, 2, 2])
        ve2 = sb("ve2", [P, 2])
        rs2 = sb("rs2", [P, 2])
        row = [sb(f"row{i}", [P, 2, ROW]) for i in range(2)]
        x2_hi = sb("x2_hi", [P, 2, T], F16)
        x2_lo = sb("x2_lo", [P, 2, T], F16)
        th = sb("th", [I2, 2 * T])
        t1 = sb("t1", [I2, 2 * T])
        hs = sb("hs", [I2, 2, T])
        y = [sb(f"y{i}", [P, 2, H]) for i in range(2)]
        gmax = sb("gmax", [P, 2])
        gneg = sb("gneg", [P, 2])
        gsum = sb("gsum", [P, 2])
        grec = sb("grec", [P, 2])
        ex = sb("ex", [P, 2, 72])
        top = sb("top", [P, 2, 8])
        top6 = sb("top6", [P, 2, 8])
        marked = sb("marked", [P, 2, 72])
        chosen = [sb(f"chosen{i}", [P, 2, E], BF16) for i in range(2)]
        before = [sb(f"before{i}", [P, E], BF16) for i in range(2)]
        both = sb("both", [P, E], BF16)
        pos_f = sb("pos_f", [P, 2 * E])
        pos_i = sb("pos_i", [P, 2 * E], I32)
        pos_lo = sb("pos_lo", [P, 2 * E], I32)
        pos_hi = sb("pos_hi", [P, 2 * E], I32)
        tile_no = sb("tile_no", [P, 2])
        hi_hot = sb("hi_hot", [P, 2, E, 8], BF16)
        lo_hot = sb("lo_hot", [P, 2, E, 8], BF16)
        tok_hot = sb("tok_hot", [P, 2, E, 2, 8], BF16)
        table = sb("table", [P, 4, 16, 16])
        tab_s = sb("tab_s", [P, 4, 16])
        tab_t = sb("tab_t", [P, 4, 8])
        tab_e = sb("tab_e", [P, 4, 8])
        tab_u = sb("tab_u", [P, 4, 8])
        tab_r = sb("tab_r", [PAIRS, P])
        slot_tok = sb("slot_tok", [P, PAIRS], U32)
        slot_f = sb("slot_f", [P, PAIRS])
        idx_g = sb("idx_g", [P, U], U32)
        idx_s = sb("idx_s", [P, U], U32)
        twice = sb("twice", [P, U])
        picked = [sb(f"picked{i}", [PAIRS, P]) for i in range(2)]
        zero = sb("zero", [P, ROW])
        w_gu = [sb(f"w_gu{i}", [P, 2, 2, 2 * I2]) for i in range(U)]
        w_dn = [sb(f"w_dn{i}", [I2, 2, H]) for i in range(U)]
        spare = x_all[:].rearrange("p s m -> p (s m)")
        g_x = [spare[:, ROW * i:ROW * i + ROW] for i in range(U)]
        e_0 = U * ROW
        g_xt = [spare[:, e_0 + H * i:e_0 + H * i + H].rearrange("p (c s) -> p c s", c=2) for i in range(2)]
        e_o = [spare[:, e_0 + 2 * H + H * i:e_0 + 3 * H + H * i] for i in range(4)]
        same = [spare[:, e_0 + 6 * H + H * i:e_0 + 7 * H + H * i].rearrange("p (e s) -> p e s", e=2) for i in range(4)]
        e_th = [sb(f"e_th{i}", [P, I2]) for i in range(2)]
        e_t1 = [sb(f"e_t1{i}", [P, I2]) for i in range(2)]
        e_h = [sb(f"e_h{i}", [P, I2]) for i in range(2)]
        e_ht = [spare[0:I2, e_0 + 10 * H + H * i:e_0 + 11 * H + H * i].rearrange("p (e s) -> p e s", e=2) for i in range(2)]

        x_d = x.rearrange("b (t p) h -> b p t h", p=P)
        out_t = out.rearrange("b (t p) h -> b p t h", p=P)
        out_rows = out.rearrange("b t h -> (b t) h")
        rows_t = rows_d[0:NT, :].rearrange("(b t p) h -> b p t h", t=2, p=P)

        def pairs_of_blocks(ap):
            return ap.rearrange("p (s d) -> p s d", d=D)

        USES = ["xtr", "pos", "otr0", "otr1", "q", "k", "ontr", "var", "wo", "vtr", "x2tr",
                "v", "sg", "su", "gate", "so", "cmp0", "cmp1"]
        STAGE = {"xtr": 1, "q": 1, "k": 1, "var": 1, "vtr": 1, "v": 1, "otr0": -1, "otr1": -1, "ontr": -1,
                 "wo": -1, "x2tr": -2, "sg": -2, "su": -2, "gate": -2, "so": -2, "pos": -3, "cmp0": -3, "cmp1": -3}

        def g_bank(use):
            return G_BANK[USES.index(use) % 3]

        def active(s, offset):
            return not isinstance(s.n, int) or 0 <= s.n + offset < NB

        def bank_free(pe, s, use):
            i = USES.index(use)
            for back in range(1, 7):
                j = i - 3 * back
                prev, steps = USES[j % 18], (0 if j >= 0 else 1)
                b = s.n - steps + STAGE[prev]
                if isinstance(b, int) and not 0 <= b < NB:
                    continue
                pe.wait_ge(sem(prev + "_read"), b + 1)
                return

        block = ctx.enter_context(nc.Block())

        def pipeline(eng, body, first=-2):
            for n in range(first, 4):
                body(Step(n, n % 2))
            with eng.Fori(2, 6) as i:
                body(Step(2 * i, 0))
                body(Step(2 * i + 1, 1))
            for n in range(12, NB + 3):
                body(Step(n, n % 2))

        def load_expert(sp, pair, u):
            sp.dma_start(w_gu[u][:], wgu[bass.ds(2 * pair, 2)].rearrange("e (c p) m -> p e c m", p=P)).then_inc(sem(f"w_expert{u}"), 16)
            sp.dma_start(w_dn[u][:], wdn[bass.ds(2 * pair, 2)].rearrange("e p h -> p e h")).then_inc(sem(f"w_expert{u}"), 16)

        def behind(i, u, lag):
            i, u = (i, u - lag) if u >= lag else (i - 1, u - lag + U)
            if isinstance(i, int) and not 0 <= i < PAIRS // U:
                return None
            return U * i + u, u, i

        def expert_steps(eng, step, lag):
            for u in range(U):
                step(0, u)
            with eng.Fori(1, PAIRS // U) as i:
                for u in range(U):
                    step(i, u)
            for u in range(lag):
                step(PAIRS // U, u)

        @block.sync
        def _(sp):
            sp.dma_start(cst[:], const).then_inc(sem("const_in"), 16)
            sp.dma_start(gb[:, 0, :], gamma.rearrange("(o d) -> o d", o=1).to_broadcast([P, D])).then_inc(sem("w_in"), 16)
            sp.dma_start(gb[:, 1, :], beta.rearrange("(o d) -> o d", o=1).to_broadcast([P, D])).then_inc(sem("w_in"), 16)
            for i, w in enumerate((wq, wk, wv)):
                sp.dma_start(w_raw[:, :, 256 * i:256 * i + 256],
                             w.rearrange("(c p) m -> p c m", p=P)).then_inc(sem("w_in"), 16)
            for b in range(2):
                sp.dma_start(x_all[:, 2 * b:2 * b + 2, :], x_d[b]).then_inc(sem(f"x_in{b}"), 16)
            sp.dma_start(x_all[:, 4:6, :], x_d[2]).then_inc(sem("x_in"), 16)
            sp.dma_start(wo_s[:], wo.rearrange("(c p) m -> p c m", p=P)).then_inc(sem("w_in"), 16)
            for i, (w, m) in enumerate(((wsg, 192), (wsu, 192), (wg, 64))):
                sp.dma_start(s_raw[:, :, 192 * i:192 * i + m],
                             w.rearrange("(c p) m -> p c m", p=P)).then_inc(sem("w_in"), 16)
            sp.dma_start(wsd_s[:], wsd.rearrange("(m p) h -> p m h", p=I2)).then_inc(sem("w_in"), 16)
            sp.wait_ge(sem("zeroed"), 1)
            sp.dma_start(rows_d[NT:ROWS, :], zero[:]).then_inc(sem("zero_out"), 16)
            for i in range(U):
                load_expert(sp, i, i)

            def body(s):
                if active(s, 3) and not (isinstance(s.n, int) and s.n < 0):
                    b, _p = s.batch(3)
                    sp.wait_ge(sem("x_in"), 16 * (s.n + 1))
                    sp.dma_start(x_all[:, bass.ds(2 * b, 2), :],
                                 x_d[bass.ds(b, 1)].rearrange("o p t h -> p (o t) h")).then_inc(sem("x_in"), 16)
                if active(s, -3):
                    b, p = s.batch(-3)
                    sp.wait_ge(sem("so_read"), b + 1)
                    sp.dma_start(out_t[bass.ds(b, 1)].rearrange("o p t h -> p (o t) h"), y[p][:]).then_inc(sem("y_out"), 16)
                    sp.wait_ge(sem("row"), b + 1)
                    sp.dma_start(rows_t[bass.ds(b, 1)].rearrange("o p t h -> p (o t) h"), row[p][:]).then_inc(sem("row_out"), 16)
                if active(s, 1):
                    b, p = s.batch(1)
                    plain_wait(sp, sem("ready"), 32 * (b - 1), 16 * (b - 1), b + 1)
                    sp.wait_ge(sem("q_read"), b + 1)
                    need(sp, sem("q_in"), 32 * (b - 1))
                    to = q_stack_d[p].rearrange("(c h) d part t -> (h d) c (part t)", c=2)
                    sp.dma_start(to, q_hl[p][:].rearrange("p c part t -> p c (part t)")).then_inc(sem("q_out"), 16)
                    sp.wait_ge(sem("k_read"), b + 1)
                    need(sp, sem("k_in"), 16 * (b - 1))
                    to = k_stack_d[p].rearrange("(c h) d rep part t -> rep (h d) c (part t)", c=2)
                    for rep in range(2):
                        sp.dma_start(to[rep], k_hl[p][:].rearrange("p c part t -> p c (part t)")).then_inc(sem("k_out"), 16)
                    plain_wait(sp, sem("ready"), 32 * (b + 1), 16 * (b + 1), b - 1)
                    need(sp, sem("score7"), b - 1)
                    sp.wait_ge(sem("q_out"), 16 * (b + 1))
                    back = q_stack_d[p].rearrange("(g hh) d part t -> (hh d part) g t", hh=2)
                    for rep in range(2):
                        sp.dma_start(q_st[p][rep:P:2], back).then_inc(sem("q_in"), 16)
                    sp.wait_ge(sem("k_out"), 32 * (b + 1))
                    back = k_stack_d[p].rearrange("(g hh) d rep part t -> (hh d rep part) g t", hh=2)
                    sp.dma_start(k_st[p][:], back).then_inc(sem("k_in"), 16)

            pipeline(sp, body)

            sp.wait_ge(sem("tab_u"), 1)
            sp.dma_start(table_d.rearrange("(g p b) -> p g b", g=4, p=P), tab_u[:]).then_inc(sem("table_out"), 16)
            sp.wait_ge(sem("table_out"), 16)
            sp.dma_start(tab_r[:], table_d.rearrange("(g p) -> g p", p=P)).then_inc(sem("table_in"), 16)
            with sp.Fori(0, PAIRS // U - 1) as i:
                for u in range(U):
                    plain_wait(sp, sem("ready"), U * i + u + 1)
                    need(sp, sem("e_down"), U * i + u + 1)
                    load_expert(sp, U * i + U + u, u)
            sp.wait_ge(sem("added"), 16 * PAIRS)

        @block.tensor
        def _(pe):
            def split3(o, w, xx, first, last):
                pe.matmul(o, w[0], xx[0], start=first, stop=False)
                pe.matmul(o, w[1], xx[0], start=False, stop=False)
                return pe.matmul(o, w[0], xx[1], start=False, stop=last)

            def scores(s, g):
                b, p = s.batch(0)
                if g == 0:
                    pe.wait_ge(sem("q_in"), 32 * (b + 1))
                    pe.wait_ge(sem("k_in"), 16 * (b + 1))
                for h in range(4 * g, 4 * g + 4):
                    if h % 2 == 0:
                        pair = h // 2
                        need(pe, sem(f"square{(pair - 2) % 8}"), b + 1 if pair >= 2 else b)
                    q = 64 * (h % 2)
                    o = S_BANK[h % 4]
                    kk, qq = k_st[p][q:q + 64, h // 2, :], q_st[p][q:q + 64, h // 2, :]
                    pe.matmul(o[:, 0:128], kk[:, 128:256], qq[:, 128:256], start=True, stop=True, tile_position=(q, 0))
                    mm = pe.matmul(o[:, 128:384], kk[:, 0:128], qq, start=True, stop=True, tile_position=(q, 0))
                    if h % 2:
                        mm.then_inc(sem(f"score{h // 2}"), 1)

            def values(s, g):
                b, p = s.batch(0)
                if g == 0:
                    pe.wait_ge(sem("v_read"), b + 1)
                pe.wait_ge(sem(f"masked{g}"), b + 1)
                if g % 2 == 0:
                    need(pe, sem("o_read1") if g == 0 else sem("o_read0"), b if g == 0 else b + 1)
                c = 256 * (g % 2)
                for j in range(4):
                    h = 4 * g + j
                    pe.matmul(O_BANK[32 * j:32 * j + 32, c:c + 256], v_w[p][:, 0, h, :], a_sq[:, h % 8, 128:384],
                              start=True, stop=False, tile_position=(0, 32 * j), skip_group_check=True)
                for j in range(4):
                    h = 4 * g + j
                    mm = pe.matmul(O_BANK[32 * j:32 * j + 32, c + 128:c + 256], v_w[p][:, 1, h, :], a_sq[:, h % 8, 0:128],
                                   start=False, stop=True, tile_position=(0, 32 * j), skip_group_check=True)
                mm.then_inc(sem(f"value{g}"), 1)

            def transposes(s, use, src, after):
                bank_free(pe, s, use)
                pe.wait_ge(*after)
                o = g_bank(use)
                for c in range(2):
                    for t in range(2):
                        tr = pe.transpose(o[:, 256 * c + 128 * t:256 * c + 128 * t + 128], src[:, t, 128 * c:128 * c + 128], ident)
                tr.then_inc(sem(use), 1)

            def project(s, use, first_col):
                b, p = s.batch(1)
                bank_free(pe, s, use)
                pe.wait_ge(sem("xtr_read"), b + 1)
                for m in range(2):
                    o = g_bank(use)[:, 256 * m:256 * m + 256]
                    pe.matmul(o, bias_w[:].rearrange("p i d -> p (i d)"), frac_b[:], start=True, stop=False)
                    for c in range(2):
                        cols = slice(first_col + 128 * m, first_col + 128 * m + 128)
                        mm = split3(o, (w_hi[:, c, cols], w_lo[:, c, cols]), (x_hi[:, c, :], x_lo[:, c, :]), False, c == 1)
                mm.then_inc(sem(use), 1)

            def body(s):
                if active(s, 1):
                    b, p = s.batch(1)
                    transposes(s, "xtr", xn[p], (sem("xn"), b + 1))
                if active(s, 0):
                    scores(s, 0)
                if active(s, -3):
                    b, p = s.batch(-3)
                    bank_free(pe, s, "pos")
                    pe.wait_ge(sem("chosen"), b + 1)
                    pe.wait_ge(sem("before"), b + 1)
                    o = g_bank("pos")
                    pe.matmul(o[:, 0:64], one_b[:], before[p][:], start=True, stop=False)
                    pe.matmul(o[:, 0:64], tri_b[:], chosen[p][:, 0, :], start=False, stop=True)
                    pe.matmul(o[:, 64:128], one_b[:], before[p][:], start=True, stop=False)
                    pe.matmul(o[:, 64:128], one_b[:], chosen[p][:, 0, :], start=False, stop=False)
                    pe.matmul(o[:, 64:128], tri_b[:], chosen[p][:, 1, :], start=False, stop=True).then_inc(sem("pos"), 1)
                if active(s, -1):
                    b, p = s.batch(-1)
                    for t in range(2):
                        bank_free(pe, s, f"otr{t}")
                        pe.wait_ge(sem("o_read1"), b + 1)
                        for g in range(4):
                            tr = pe.transpose(g_bank(f"otr{t}")[:, 128 * g:128 * g + 128], o_t[:, g, 128 * t:128 * t + 128], ident)
                        tr.then_inc(sem(f"otr{t}"), 1)
                if active(s, 0):
                    scores(s, 1)
                if active(s, 1):
                    project(s, "q", 0)
                if active(s, 0):
                    values(s, 0)
                if active(s, 1):
                    project(s, "k", 256)
                if active(s, -1):
                    b, p = s.batch(-1)
                    transposes(s, "ontr", o_n, (sem("otr1_read"), b + 1))
                if active(s, 0):
                    scores(s, 2)
                if active(s, 1):
                    b, p = s.batch(1)
                    bank_free(pe, s, "var")
                    pe.wait_ge(sem("q_sq"), b + 1)
                    pe.wait_ge(sem("k_sq"), b + 1)
                    for j in range(4):
                        mm = pe.matmul(g_bank("var")[32 * j:32 * j + 32, 0:256], blk, (q_sq, k_sq)[j // 2][:, j % 2, :],
                                       start=True, stop=True, tile_position=(0, 32 * j))
                    mm.then_inc(sem("var"), 1)
                if active(s, 0):
                    values(s, 1)
                if active(s, -1):
                    b, p = s.batch(-1)
                    bank_free(pe, s, "wo")
                    pe.wait_ge(sem("ontr_read"), b + 1)
                    for t in range(2):
                        for c in range(2):
                            mm = pe.matmul(g_bank("wo")[:, 256 * t:256 * t + 256], o_nt[:, c, 128 * t:128 * t + 128],
                                           wo_s[:, c, :], start=c == 0, stop=c == 1)
                    mm.then_inc(sem("wo"), 1)
                if active(s, 1):
                    b, p = s.batch(1)
                    bank_free(pe, s, "vtr")
                    pe.wait_ge(sem("var_read"), b + 1)
                    for t in range(2):
                        tr = pe.transpose(g_bank("vtr")[:, 128 * t:128 * t + 128], var_t[:, 128 * t:128 * t + 128], ident)
                    tr.then_inc(sem("vtr"), 1)
                if active(s, -2):
                    b, p = s.batch(-2)
                    transposes(s, "x2tr", row[p], (sem("x2n"), b + 1))
                if active(s, 0):
                    scores(s, 3)
                if active(s, 1):
                    b, p = s.batch(1)
                    bank_free(pe, s, "v")
                    for t in range(2):
                        for c in range(2):
                            tok = slice(128 * t, 128 * t + 128)
                            mm = split3(g_bank("v")[:, 256 * t:256 * t + 256], (x_hi[:, c, tok], x_lo[:, c, tok]),
                                        (w_hi[:, c, 512:768], w_lo[:, c, 512:768]), c == 0, c == 1)
                    mm.then_inc(sem("v"), 1)
                if active(s, 0):
                    values(s, 2)
                if active(s, -2):
                    b, p = s.batch(-2)
                    for use, first in (("sg", 0), ("su", 192)):
                        bank_free(pe, s, use)
                        pe.wait_ge(sem("x2tr_read"), b + 1)
                        for m in range(2):
                            for c in range(2):
                                cols = slice(first + I2 * m, first + I2 * m + I2)
                                mm = split3(g_bank(use)[0:I2, 256 * m:256 * m + 256], (s_hi[:, c, cols], s_lo[:, c, cols]),
                                            (x2_hi[:, c, :], x2_lo[:, c, :]), c == 0, c == 1)
                        mm.then_inc(sem(use), 1)
                    bank_free(pe, s, "gate")
                    for t in range(2):
                        for c in range(2):
                            tok = slice(128 * t, 128 * t + 128)
                            mm = split3(g_bank("gate")[:, 64 * t:64 * t + 64], (x2_hi[:, c, tok], x2_lo[:, c, tok]),
                                        (s_hi[:, c, 384:448], s_lo[:, c, 384:448]), c == 0, c == 1)
                    mm.then_inc(sem("gate"), 1)
                if active(s, 0):
                    values(s, 3)
                if active(s, -2):
                    b, p = s.batch(-2)
                    bank_free(pe, s, "so")
                    pe.wait_ge(sem("su_read"), b + 1)
                    for t in range(2):
                        for m in range(2):
                            mm = pe.matmul(g_bank("so")[:, 256 * t:256 * t + 256], hs[:, m, 128 * t:128 * t + 128],
                                           wsd_s[:, m, :], start=m == 0, stop=m == 1)
                    mm.then_inc(sem("so"), 1)
                if active(s, -3):
                    b, p = s.batch(-3)
                    for half in range(2):
                        use = f"cmp{half}"
                        bank_free(pe, s, use)
                        pe.wait_ge(sem("tok_hot"), b + 1)
                        for gr in range(2):
                            ex16 = slice(32 * half + 16 * gr, 32 * half + 16 * gr + 16)
                            for t in range(2):
                                mm = pe.matmul(g_bank(use)[:, 256 * gr:256 * gr + 256],
                                               hi_hot[:, t, ex16, :].rearrange("p e a -> p (e a)"),
                                               tok_hot[:, t, ex16, :, :].rearrange("p e w b -> p (e w b)"),
                                               start=t == 0, stop=t == 1)
                        mm.then_inc(sem(use), 1)

            pe.wait_ge(sem("const_in"), 16)
            pe.wait_ge(sem("w_ready"), 2)
            pe.wait_ge(sem("w_in"), 16 * 10)
            pipeline(pe, body)

            def gather_t(pair, u, i):
                pe.wait_ge(sem(f"gathered{u % 4}"), 16 * (2 * i + u // 4 + 1))
                need(pe, sem("g_xt"), pair - 1)
                o = bank[u % 2]
                for c in range(2):
                    tr = pe.transpose(o[:, 128 * c:128 * c + 128], g_x[u][:, 128 * c:128 * c + 128], ident)
                tr.then_inc(sem("gtr"), 1)

            def tokens(pair, u, i):
                need(pe, sem("same"), pair)
                pe.wait_ge(sem("picked"), pair + 1)
                pe.matmul(bank[7][:, 0:P], cst[0:PAIRS, C_ONE:C_ONE + P], picked[u % 2][:],
                          start=True, stop=True).then_inc(sem("tokens"), 1)

            def gate_up(pair, u, i):
                pe.wait_ge(sem("g_xt"), pair + 1)
                pe.wait_ge(sem(f"w_expert{u}"), 32 * (i + 1))
                need(pe, sem("e_h"), pair - 1)
                o = bank[2 + u % 2]
                for c in range(2):
                    for e in range(2):
                        mm = pe.matmul(o[64 * e:64 * e + 64, 0:2 * I2], g_xt[u % 2][:, c, 64 * e:64 * e + 64], w_gu[u][:, e, c, :],
                                       start=c == 0, stop=c == 1, tile_position=(0, 64 * e), skip_group_check=True)
                mm.then_inc(sem("gu"), 1)

            def hidden_t(pair, u, i):
                pe.wait_ge(sem("e_h"), pair + 1)
                pe.wait_ge(sem("same"), pair + 1)
                need(pe, sem("e_ht"), pair - 1)
                pe.matmul(bank[4 + u % 2][0:I2, 0:2 * P], e_h[u % 2][:], same[u % 4].rearrange("p e s -> p (e s)"),
                          start=True, stop=True).then_inc(sem("htr"), 1)

            def down(pair, u, i):
                pe.wait_ge(sem("e_ht"), pair + 1)
                need(pe, sem("e_o"), pair)
                for e in range(2):
                    mm = pe.matmul(bank[6][:, 0:H], e_ht[u % 2][:, e, :], w_dn[u][:, e, :], start=e == 0, stop=e == 1)
                mm.then_inc(sem("e_down"), 1)

            def expert_step(i, u):
                for stage, lag in ((gather_t, 1), (gate_up, 2), (tokens, 1), (hidden_t, 3), (down, 4)):
                    at = behind(i, u, lag)
                    if at:
                        stage(*at)

            pe.wait_ge(sem("o_read1"), NB)
            pe.wait_ge(sem("cmp0_read"), NB)
            pe.wait_ge(sem("cmp1_read"), NB)
            pe.wait_ge(sem("pos_read"), NB)
            pe.wait_ge(sem("table_in"), 16)
            pe.transpose(bank[0][:, 0:PAIRS], tab_r[:], ident[0:PAIRS, 0:PAIRS]).then_inc(sem("table_t"), 1)
            pe.wait_ge(sem("slots"), 2)
            expert_steps(pe, expert_step, 4)

        @block.scalar
        def _(act):
            def squares(s, pair):
                b, p = s.batch(0)
                act.wait_ge(sem(f"score{pair}"), b + 1)
                need(act, sem(f"value{(pair // 2 - 2) % 4}"), b + 1 if pair >= 4 else b)
                for h in (2 * pair, 2 * pair + 1):
                    sq = act.activation(a_sq[:, h % 8, :], S_BANK[h % 4][:, 0:384], ACT.Square)
                sq.then_inc(sem(f"square{pair}"), 1)

            def out_copy(s, half):
                b, p = s.batch(0)
                act.wait_ge(sem(f"value{2 * half + 1}"), b + 1)
                if half == 0:
                    need(act, sem("otr1"), b)
                act.copy(o_t[:, 2 * half:2 * half + 2, :].rearrange("p g t -> p (g t)"), O_BANK[:]).then_inc(sem(f"o_read{half}"), 1)

            def flat(ap):
                return ap.rearrange("p c t -> p (c t)")

            def body(s):
                if active(s, 1):
                    b, p = s.batch(1)
                    act.wait_ge(sem("xtr"), b + 1)
                    need(act, sem("v"), b)
                    act.copy(flat(x_hi[:]), g_bank("xtr")[:]).then_inc(sem("x_hi"), 1)
                if active(s, 0):
                    squares(s, 0)
                    squares(s, 1)
                if active(s, 0):
                    squares(s, 2)
                    squares(s, 3)
                if active(s, 1):
                    b, p = s.batch(1)
                    for use, hl, sq in (("q", q_hl, q_sq), ("k", k_hl, k_sq)):
                        act.wait_ge(sem(use), b + 1)
                        need(act, sem(use + "_out"), (16 if use == "q" else 32) * (b - 1))
                        if use == "q":
                            need(act, sem("var"), b)
                        act.copy(hl[p][:, :, 0, :], g_bank(use)[:].rearrange("p (c t) -> p c t", c=2)).then_inc(sem(use + "_hi"), 1)
                        act.activation(flat(sq[:]), g_bank(use)[:], ACT.Square).then_inc(sem(use + "_sq"), 1)
                if active(s, -1):
                    b, p = s.batch(-1)
                    act.wait_ge(sem("ontr"), b + 1)
                    need(act, sem("wo"), b)
                    act.copy(flat(o_nt[:]), g_bank("ontr")[:]).then_inc(sem("ontr_read"), 1)
                if active(s, 0):
                    squares(s, 4)
                    squares(s, 5)
                    out_copy(s, 0)
                if active(s, 1):
                    b, p = s.batch(1)
                    act.wait_ge(sem("var"), b + 1)
                    need(act, sem("vtr"), b)
                    act.copy(var_t[:], g_bank("var")[:, 0:256]).then_inc(sem("var_read"), 1)
                if active(s, -2):
                    b, p = s.batch(-2)
                    act.wait_ge(sem("x2tr"), b + 1)
                    need(act, sem("gate"), b)
                    act.copy(flat(x2_hi[:]), g_bank("x2tr")[:]).then_inc(sem("x2_hi"), 1)
                if active(s, 0):
                    squares(s, 6)
                    squares(s, 7)
                if active(s, -2):
                    b, p = s.batch(-2)
                    act.wait_ge(sem("sg"), b + 1)
                    need(act, sem("sg_read"), b)
                    act.activation(th[:], g_bank("sg")[0:I2, :], ACT.Tanh, scale=0.5).then_inc(sem("th"), 1)
                    act.wait_ge(sem("gneg"), b + 1)
                    need(act, sem("chosen"), b)
                    need(act, sem("row"), b)
                    for t in range(2):
                        e = act.activation(ex[:, t, 0:64], g_bank("gate")[:, 64 * t:64 * t + 64], ACT.Exp,
                                           bias=gneg[:, t:t + 1], accum_out=gsum[:, t:t + 1])
                    e.then_inc(sem("gate_read"), 1)
                if active(s, 0):
                    out_copy(s, 1)

            act.wait_ge(sem("ready"), 1)
            pipeline(act, body)

            def gathered_copy(pair, u, i):
                act.wait_ge(sem("gtr"), pair + 1)
                need(act, sem("gu"), pair - 1)
                act.copy(g_xt[u % 2].rearrange("p c s -> p (c s)"), bank[u % 2][:, 0:256]).then_inc(sem("g_xt"), 1)

            def gate_tanh(pair, u, i):
                act.wait_ge(sem("gu"), pair + 1)
                need(act, sem("e_t1"), pair - 1)
                act.activation(e_th[u % 2][:], bank[2 + u % 2][:, 0:I2], ACT.Tanh, scale=0.5).then_inc(sem("e_th"), 1)

            def hidden_copy(pair, u, i):
                act.wait_ge(sem("htr"), pair + 1)
                need(act, sem("e_down"), pair - 1)
                act.copy(e_ht[u % 2].rearrange("p e s -> p (e s)"), bank[4 + u % 2][0:I2, 0:2 * P]).then_inc(sem("e_ht"), 1)

            def output_copy(pair, u, i):
                act.wait_ge(sem("e_down"), pair + 1)
                need(act, sem("added"), 16 * (pair - 3))
                act.copy(e_o[u % 4], bank[6][:, 0:H]).then_inc(sem("e_o"), 1)

            def expert_step(i, u):
                for stage, lag in ((gathered_copy, 1), (gate_tanh, 2), (hidden_copy, 3), (output_copy, 4)):
                    at = behind(i, u, lag)
                    if at:
                        stage(*at)

            expert_steps(act, expert_step, 4)

        @block.gpsimd
        def _(pool):
            pool.memset(zero[:], 0.0).then_inc(sem("zeroed"), 1)

            def masks(s, pair):
                b, p = s.batch(0)
                plain_wait(pool, sem("ready"), b + 1)
                need(pool, sem(f"square{pair}"), b + 1)
                h = 2 * pair % 8
                a = a_sq[:, h:h + 2, 0:2 * P]
                m = pool.affine_select(out=a, in_=a, pattern=[[0, 2], [0, 2], [1, P]], compare_op=ALU.is_ge, fill=0.0,
                                       base=0, channel_multiplier=-1)
                if pair % 2:
                    m.then_inc(sem(f"masked{pair // 2}"), 1)

            def body(s):
                if active(s, 2):
                    b, p = s.batch(2)
                    pool.wait_ge(sem("ve1"), b + 1)
                    need(pool, sem("xn"), b)
                    pool.tensor_tensor(rs1[:], ve1[:], mhalf[:], ALU.pow).then_inc(sem("rs1"), 1)
                if active(s, 0):
                    for pair in range(6):
                        masks(s, pair)
                if active(s, -1):
                    b, p = s.batch(-1)
                    pool.wait_ge(sem("ve2"), b + 1)
                    need(pool, sem("x2n"), b)
                    pool.tensor_tensor(rs2[:], ve2[:], mhalf[:], ALU.pow).then_inc(sem("rs2"), 1)
                if active(s, 0):
                    for pair in range(6, 8):
                        masks(s, pair)

            pool.wait_ge(sem("ready"), 1)
            pipeline(pool, body)

            pool.wait_ge(sem("slots"), 2)
            pool.wait_ge(sem("row_out"), 16 * NB)
            pool.wait_ge(sem("y_out"), 16 * NB)
            pool.wait_ge(sem("zero_out"), 16)

            AHEAD = 6

            def gather(pair, u, i):
                need(pool, sem("e_h"), pair - U + 1)
                need(pool, sem(f"gathered{u % 4}"), 16 * (2 * i + u // 4))
                pool.tensor_copy(idx_g[:, u:u + 1], slot_tok[:, bass.ds(pair, 1)]).then_inc(sem("idx"), 1)
                plain_wait(pool, sem("ready"), pair + 1)
                pool.wait_ge(sem("idx"), pair + 1)
                pool.indirect_dma_start(out=g_x[u], out_offset=None, in_=rows_d[:, :],
                                        in_offset=bass.IndirectOffsetOnAxis(ap=idx_g[:, u:u + 1], axis=0)).then_inc(sem(f"gathered{u % 4}"), 16)

            def scatter(pair, u, i):
                plain_wait(pool, sem("ready"), pair + 1, 16 * pair)
                pool.wait_ge(sem("idx_s"), pair + 1)
                pool.wait_ge(sem("e_o"), pair + 1)
                need(pool, sem("added"), 16 * pair)
                pool.indirect_dma_start(out=out_rows, out_offset=bass.IndirectOffsetOnAxis(ap=idx_s[:, u:u + 1], axis=0),
                                        in_=e_o[u % 4], in_offset=None, compute_op=ALU.add,
                                        bounds_check=NT - 1, oob_is_err=False).then_inc(sem("added"), 16)

            def expert_step(i, u):
                at = behind(i, u, AHEAD)
                if at:
                    scatter(*at)
                at = behind(i, u, 0)
                if at:
                    gather(*at)

            expert_steps(pool, expert_step, AHEAD)

        @block.vector
        def _(dve):
            done = [0]

            def chain(ins):
                done[0] += 1
                ins.then_inc(sem("setup"), 1)
                dve.wait_ge(sem("setup"), done[0])

            for i in range(2):
                chain(dve.memset(v_w[i][:].rearrange("p t h c -> p (t h c)"), 0.0))
            chain(dve.memset(mhalf[:], -0.5))
            chain(dve.memset(frac_b[:], 1.0 / 64))
            chain(dve.memset(ex[:].rearrange("p t e -> p (t e)"), -2.0))
            chain(dve.memset(top6[:].rearrange("p t e -> p (t e)"), -2.0))
            chain(dve.memset(before[0][:], 0.0))
            chain(dve.memset(table[:].rearrange("p g e w -> p (g e w)"), 0.0))
            chain(dve.memset(tile_no[:, 0:1], -2.0))
            chain(dve.memset(tile_no[:, 1:2], -1.0))
            dve.wait_ge(sem("const_in"), 16)
            chain(dve.tensor_copy(tri_b[:], cst[:, C_TRI:C_TRI + P]))
            chain(dve.tensor_copy(one_b[:], cst[:, C_ONE:C_ONE + P]))
            chain(dve.memset(b_mean[:], 0.0))
            dve.memset(b_c[:], 0.0).then_inc(sem("ready"), 1)
            dve.wait_ge(sem("ready"), 1)

            def ln1(b, p, x_pair):
                for t in range(2):
                    st = dve.bn_stats(st1[:, t, :], x_pair[:, t, :])
                st.then_inc(sem("st1"), 1)
                plain_wait(dve, sem("ready"), b + 1)
                need(dve, sem("st1"), b + 1)
                for t in range(2):
                    ag = dve.bn_aggr(mv1[:, t, :], st1[:, t, :])
                ag.then_inc(sem("mv1"), 1)
                dve.wait_ge(sem("mv1"), b + 1)
                need(dve, sem("rs1"), b)
                dve.tensor_scalar(ve1[:], mv1[:, :, 1], EPS, None, ALU.add).then_inc(sem("ve1"), 1)

            def ln1_apply(b, p, x_pair):
                dve.wait_ge(sem("rs1"), b + 1)
                need(dve, sem("xtr"), b - 1)
                for t in range(2):
                    n = dve.tensor_scalar(xn[p][:, t, :], x_pair[:, t, :], mv1[:, t, 0:1], rs1[:, t:t + 1], ALU.subtract, ALU.mult)
                n.then_inc(sem("xn"), 1)

            def flat(ap):
                return ap.rearrange("p c t -> p (c t)")

            def positions(s):
                b, p = s.batch(-3)
                need(dve, sem("tok_hot"), b)
                dve.tensor_scalar(tile_no[:], tile_no[:], 2.0, None, ALU.add).then_inc(sem("tile_no"), 1)
                ch = chosen[p][:].rearrange("p t e -> p (t e)")
                dve.wait_ge(sem("pos"), b + 1)
                dve.scalar_tensor_tensor(pos_f[:], ch, -1024.0, g_bank("pos")[:, 0:128], ALU.mult, ALU.add).then_inc(sem("pos_read"), 1)
                dve.tensor_tensor(both[:], chosen[p][:, 0, :], chosen[p][:, 1, :], ALU.add).then_inc(sem("both"), 1)
                dve.wait_ge(sem("both"), b + 1)
                dve.tensor_tensor(before[1 - p][:], before[p][:], both[:], ALU.add).then_inc(sem("before"), 1)
                dve.wait_ge(sem("pos_read"), b + 1)
                dve.tensor_scalar(pos_i[:], pos_f[:], 1024.0, None, ALU.add).then_inc(sem("pos_i"), 1)

            def one_hots(s):
                b, p = s.batch(-3)
                dve.wait_ge(sem("pos_i"), b + 1)
                dve.tensor_scalar(pos_lo[:], pos_i[:], 7, None, ALU.bitwise_and)
                dve.tensor_scalar(pos_hi[:], pos_i[:], 3, None, ALU.arith_shift_right).then_inc(sem("digits"), 1)
                dve.wait_ge(sem("digits"), b + 1)
                need(dve, sem("cmp1"), b)
                digits = cst[:, C_IOTA:C_IOTA + 8].unsqueeze(1).to_broadcast([P, 2 * E, 8])
                for dst, src in ((hi_hot, pos_hi), (lo_hot, pos_lo)):
                    hot = dve.tensor_tensor(dst[:].rearrange("p t e d -> p (t e) d"), src[:].unsqueeze(2).to_broadcast([P, 2 * E, 8]),
                                            digits, ALU.is_equal)
                hot.then_inc(sem("lo_hot"), 1)
                dve.wait_ge(sem("lo_hot"), b + 1)
                dve.wait_ge(sem("tile_no"), b + 1)
                dve.tensor_scalar(tok_hot[:, :, :, 0, :].rearrange("p t e d -> p (t e) d"),
                                  lo_hot[:].rearrange("p t e d -> p (t e) d"), cst[:, C_P1:C_P1 + 1], None, ALU.mult)
                for t in range(2):
                    th_ = dve.tensor_scalar(tok_hot[:, t, :, 1, :], lo_hot[:, t, :, :], tile_no[:, t:t + 1], None, ALU.mult)
                th_.then_inc(sem("tok_hot"), 1)

            def low_part(b, use, hi_sem, hi, lo, after_sem):
                dve.wait_ge(sem(hi_sem), b + 1)
                dve.tensor_tensor(lo, g_bank(use)[:], hi, ALU.subtract).then_inc(sem(after_sem), 1)

            def body(s):
                x_of = lambda b: x_all[:, bass.ds(2 * b, 2), :] if not isinstance(b, int) else x_all[:, 2 * b:2 * b + 2, :]
                if active(s, 1):
                    b, p = s.batch(1)
                    dve.wait_ge(sem("x_hi"), b + 1)
                    need(dve, sem("v"), b)
                    dve.tensor_tensor(flat(x_lo[:]), g_bank("xtr")[:], flat(x_hi[:]), ALU.subtract).then_inc(sem("xtr_read"), 1)
                if active(s, 2):
                    b, p = s.batch(2)
                    if isinstance(b, int) and b < 2:
                        dve.wait_ge(sem(f"x_in{b}"), 16)
                    else:
                        plain_wait(dve, sem("ready"), 16 * (b - 1))
                        dve.wait_ge(sem("x_in"), 16 * (b - 1))
                    ln1(b, p, x_of(b))
                if active(s, -3):
                    positions(s)
                if active(s, -1):
                    b, p = s.batch(-1)
                    for t in range(2):
                        dve.wait_ge(sem(f"otr{t}"), b + 1)
                        o = g_bank(f"otr{t}")[:].rearrange("p (h c) -> p h c", c=32)
                        dd = dve.tensor_tensor(den[:, t, :], o[:, :, 16], q_eps[p][:, t, :], ALU.add)
                    dd.then_inc(sem("den"), 1)
                    dve.wait_ge(sem("den"), b + 1)
                    dve.reciprocal(rec[:].rearrange("p t h -> p (t h)"), den[:].rearrange("p t h -> p (t h)")).then_inc(sem("rec"), 1)
                    dve.wait_ge(sem("rec"), b + 1)
                    need(dve, sem("ontr"), b)
                    for t in range(2):
                        o = g_bank(f"otr{t}")[:].rearrange("p (h c) -> p h c", c=32)
                        r = rec[:, t, :].unsqueeze(2).to_broadcast([P, HEADS, D])
                        on = dve.tensor_tensor(o_n[:, t, :].rearrange("p (h d) -> p h d", d=D), o[:, :, 0:16], r, ALU.mult)
                        on.then_inc(sem(f"otr{t}_read"), 1)
                if active(s, 2):
                    b, p = s.batch(2)
                    ln1_apply(b, p, x_of(b))
                if active(s, 1):
                    b, p = s.batch(1)
                    for use, hl in (("q", q_hl), ("k", k_hl)):
                        if use == "k" and active(s, -3):
                            one_hots(s)
                        dve.wait_ge(sem(use + "_hi"), b + 1)
                        dve.wait_ge(sem(use + "_sq"), b + 1)
                        dve.tensor_tensor(hl[p][:, :, 1, :], g_bank(use)[:].rearrange("p (c t) -> p c t", c=2), hl[p][:, :, 0, :],
                                          ALU.subtract).then_inc(sem(use + "_read"), 1)
                elif active(s, -3):
                    one_hots(s)
                if active(s, -1):
                    b, p = s.batch(-1)
                    dve.wait_ge(sem("wo"), b + 1)
                    xx = x_of(b)
                    dve.tensor_tensor(xx, xx, g_bank("wo")[:].rearrange("p (t h) -> p t h", t=2), ALU.add).then_inc(sem("wo_read"), 1)
                    plain_wait(dve, sem("ready"), b + 1)
                    need(dve, sem("wo_read"), b + 1)
                    for t in range(2):
                        st = dve.bn_stats(st2[:, t, :], xx[:, t, :])
                    st.then_inc(sem("st2"), 1)
                    plain_wait(dve, sem("ready"), b + 1)
                    need(dve, sem("st2"), b + 1)
                    for t in range(2):
                        ag = dve.bn_aggr(mv2[:, t, :], st2[:, t, :])
                    ag.then_inc(sem("mv2"), 1)
                    dve.wait_ge(sem("mv2"), b + 1)
                    dve.tensor_scalar(ve2[:], mv2[:, :, 1], EPS, None, ALU.add).then_inc(sem("ve2"), 1)
                if active(s, -2):
                    b, p = s.batch(-2)
                    dve.wait_ge(sem("x2_hi"), b + 1)
                    dve.tensor_tensor(flat(x2_lo[:]), g_bank("x2tr")[:], flat(x2_hi[:]), ALU.subtract).then_inc(sem("x2tr_read"), 1)
                if active(s, 1):
                    b, p = s.batch(1)
                    dve.wait_ge(sem("vtr"), b + 1)
                    g = g_bank("vtr")[:, 0:256].rearrange("p (t w m i) -> p t w m i", t=2, w=2, m=2)
                    as4 = lambda a: a.rearrange("p t (m i) -> p t m i", m=2)
                    for t in range(2):
                        gv = g[:, t, 1, :, 0:8]
                        kv = k_var[:, t, :].rearrange("p (m i) -> p m i", m=2)
                        dve.tensor_scalar(kv, gv, EPS, None, ALU.add)
                        gq = g[:, t, 0, :, 0:8]
                        qe = q_eps[p][:, t, :].rearrange("p (m i) -> p m i", m=2)
                        vr = dve.tensor_scalar(qe, gq, EPS, 16 * EPS, ALU.add, ALU.mult)
                    vr.then_inc(sem("vtr_read"), 1)
                    dve.wait_ge(sem("vtr_read"), b + 1)
                    dve.reciprocal(k_rec[:].rearrange("p t h -> p (t h)"), k_var[:].rearrange("p t h -> p (t h)")).then_inc(sem("k_rec"), 1)
                    dve.wait_ge(sem("k_rec"), b + 1)
                    need(dve, sem("value3"), b - 1)
                    for t in range(2):
                        dve.tensor_copy(v_w[p][:, t, :, 16], k_rec[:, t, :])
                    dve.wait_ge(sem("v"), b + 1)
                    for t in range(2):
                        r = k_rec[:, t, :].unsqueeze(2).to_broadcast([P, HEADS, D])
                        vv = dve.tensor_tensor(v_w[p][:, t, :, 0:16], g_bank("v")[:, 256 * t:256 * t + 256].rearrange("p (h d) -> p h d", d=D), r, ALU.mult)
                    vv.then_inc(sem("v_read"), 1)
                if active(s, -1):
                    b, p = s.batch(-1)
                    dve.wait_ge(sem("rs2"), b + 1)
                    need(dve, sem("row_out"), 16 * (b - 1))
                    xx = x_of(b)
                    for t in range(2):
                        n = dve.tensor_scalar(row[p][:, t, 0:H], xx[:, t, :], mv2[:, t, 0:1], rs2[:, t:t + 1], ALU.subtract, ALU.mult)
                    n.then_inc(sem("x2n"), 1)
                if active(s, -2):
                    b, p = s.batch(-2)
                    dve.wait_ge(sem("th"), b + 1)
                    dve.scalar_tensor_tensor(t1[:], th[:], 1.0, g_bank("sg")[0:I2, :], ALU.add, ALU.mult).then_inc(sem("sg_read"), 1)
                    dve.wait_ge(sem("sg_read"), b + 1)
                    dve.wait_ge(sem("su"), b + 1)
                    need(dve, sem("so"), b)
                    dve.scalar_tensor_tensor(flat(hs[:]), t1[:], 0.5, g_bank("su")[0:I2, :], ALU.mult, ALU.mult).then_inc(sem("su_read"), 1)
                    dve.wait_ge(sem("gate"), b + 1)
                    dve.tensor_reduce(gmax[:], g_bank("gate")[:, 0:128].rearrange("p (t e) -> p t e", t=2), AX, ALU.max).then_inc(sem("gmax"), 1)
                    dve.wait_ge(sem("gmax"), b + 1)
                    dve.tensor_scalar(gneg[:], gmax[:], -1.0, None, ALU.mult).then_inc(sem("gneg"), 1)
                    dve.wait_ge(sem("gate_read"), b + 1)
                    dve.reciprocal(grec[:], gsum[:]).then_inc(sem("grec"), 1)
                    for t in range(2):
                        mx = dve.max(top[:, t, :], ex[:, t, 0:64])
                    mx.then_inc(sem("top"), 1)
                    dve.wait_ge(sem("grec"), b + 1)
                    for t in range(2):
                        gw = dve.tensor_scalar(row[p][:, t, H:ROW], ex[:, t, 0:64], grec[:, t:t + 1], 0.5, ALU.mult, ALU.mult)
                    gw.then_inc(sem("row"), 1)
                    dve.wait_ge(sem("top"), b + 1)
                    dve.tensor_copy(top6[:, :, 0:6], top[:, :, 0:6]).then_inc(sem("top6"), 1)
                    plain_wait(dve, sem("ready"), b + 1)
                    need(dve, sem("top6"), b + 1)
                    for t in range(2):
                        mr = dve.match_replace(marked[:, t, 0:66], top6[:, t, :], ex[:, t, 0:66], -1.0)
                    mr.then_inc(sem("marked"), 1)
                    dve.wait_ge(sem("marked"), b + 1)
                    need(dve, sem("pos"), b - 1)
                    dve.tensor_scalar(chosen[p][:], marked[:, :, 0:64], 0.0, None, ALU.is_lt).then_inc(sem("chosen"), 1)
                    dve.wait_ge(sem("so"), b + 1)
                    need(dve, sem("y_out"), 16 * (b - 1))
                    dve.tensor_tensor(y[p][:], x_of(b), g_bank("so")[:].rearrange("p (t h) -> p t h", t=2), ALU.add).then_inc(sem("so_read"), 1)
                if active(s, -3):
                    b, p = s.batch(-3)
                    for half in range(2):
                        dve.wait_ge(sem(f"cmp{half}"), b + 1)
                        tb = table[:, 2 * half:2 * half + 2, :, :].rearrange("p g e w -> p (g e w)")
                        dve.tensor_tensor(tb, tb, g_bank(f"cmp{half}")[:], ALU.add).then_inc(sem(f"cmp{half}_read"), 1)

            body(Step(-2, 0))
            dve.wait_ge(sem("w_in"), 16 * 10)
            for c in range(2):
                wt = w_tmp[:, c, :].rearrange("p (h d) -> p h d", d=D)
                chain(dve.tensor_tensor(wt, w_raw[:, c, 0:512].rearrange("p (h d) -> p h d", d=D),
                                        gb[:, 0:1, :].to_broadcast([P, 32, D]), ALU.mult))
                chain(dve.tensor_reduce(w_mean[:, c, :], wt, AX, ALU.add))
                chain(dve.tensor_scalar(w_mean[:, c, :], w_mean[:, c, :], 1.0 / D, None, ALU.mult))
                wm = w_mean[:, c, :].unsqueeze(2).to_broadcast([P, 32, D])
                chain(dve.tensor_tensor(w_raw[:, c, 0:512].rearrange("p (h d) -> p h d", d=D), wt, wm, ALU.subtract))
            chain(dve.tensor_reduce(b_mean[:], gb[:, 1, :], AX, ALU.add))
            chain(dve.tensor_scalar(b_mean[:], b_mean[:], 1.0 / D, None, ALU.mult))
            chain(dve.tensor_scalar(b_c[:], gb[:, 1, :], b_mean[:, 0:1], None, ALU.subtract))
            chain(dve.tensor_copy(b_hi[:], b_c[:]))
            chain(dve.tensor_tensor(b_lo[:], b_c[:], b_hi[:], ALU.subtract))
            for half, src in enumerate((b_hi, b_lo)):
                q = slice(64 * half, 64 * half + 64)
                chain(dve.tensor_copy(bias_w[q, :, :], src[q, :].unsqueeze(1).to_broadcast([64, 8, D])))
            for hi, lo, raw in ((w_hi, w_lo, w_raw), (s_hi, s_lo, s_raw)):
                fl = lambda a: a[:].rearrange("p c m -> p (c m)")
                chain(dve.tensor_copy(fl(hi), fl(raw)))
                dve.tensor_tensor(fl(lo), fl(raw), fl(hi), ALU.subtract).then_inc(sem("w_ready"), 1)
            dve.wait_ge(sem("w_ready"), 2)
            dve.memset(both[:], 0.0).then_inc(sem("before"), 1)
            pipeline(dve, body, -1)

            dve.wait_ge(sem("cmp1_read"), NB)
            diag = cst[:, C_DIAG:C_DIAG + 16].unsqueeze(1).unsqueeze(3).to_broadcast([P, 4, 16, 16])
            chain(dve.tensor_tensor(table[:], table[:], diag, ALU.mult))
            chain(dve.tensor_reduce(tab_s[:], table[:].rearrange("p g e w -> p g w e"), AX, ALU.add))
            place, tile = tab_s[:, :, 0:8], tab_s[:, :, 8:16]
            chain(dve.scalar_tensor_tensor(tab_t[:], tile, float(P), place, ALU.mult, ALU.add))
            dump = cst[:, C_DUMP:C_DUMP + 8].unsqueeze(1).to_broadcast([P, 4, 8])
            chain(dve.scalar_tensor_tensor(tab_e[:], place, 0.0, dump, ALU.is_equal, ALU.mult))
            chain(dve.tensor_tensor(tab_t[:], tab_t[:], tab_e[:], ALU.add))
            dve.tensor_scalar(tab_u[:], tab_t[:], -1.0, None, ALU.add).then_inc(sem("tab_u"), 1)
            dve.wait_ge(sem("table_t"), 1)
            dve.tensor_copy(slot_tok[:], bank[0][:, 0:PAIRS]).then_inc(sem("slots"), 1)
            dve.tensor_copy(slot_f[:], bank[0][:, 0:PAIRS]).then_inc(sem("slots"), 1)
            dve.wait_ge(sem("slots"), 2)

            def pick(pair, u, i):
                need(dve, sem("tokens"), pair - 1)
                dve.tensor_scalar(picked[u % 2][:], tab_r[:], ident[0:PAIRS, bass.ds(pair, 1)], None, ALU.mult).then_inc(sem("picked"), 1)

            def equal_slots(pair, u, i):
                dve.wait_ge(sem("tokens"), pair + 1)
                need(dve, sem("htr"), pair - 3)
                for e in range(2):
                    half = cst[:, C_HALF + e:C_HALF + e + 1]
                    eq = dve.tensor_scalar(same[u % 4][:, e, :], bank[7][:, 0:P], slot_f[:, bass.ds(pair, 1)], half,
                                           ALU.is_equal, ALU.mult)
                eq.then_inc(sem("same"), 1)
                dve.wait_ge(sem("same"), pair + 1)
                dve.tensor_reduce(twice[:, u:u + 1], same[u % 4][:, 1, 0:64], AX, ALU.max).then_inc(sem("twice"), 1)
                dve.wait_ge(sem("twice"), pair + 1)
                need(dve, sem("added"), 16 * (pair - U + 1))
                dve.scalar_tensor_tensor(idx_s[:, u:u + 1], twice[:, u:u + 1], float(2 * NT), slot_f[:, bass.ds(pair, 1)],
                                         ALU.mult, ALU.add).then_inc(sem("idx_s"), 1)

            def hidden(pair, u, i):
                dve.wait_ge(sem("e_th"), pair + 1)
                gu = bank[2 + u % 2]
                dve.scalar_tensor_tensor(e_t1[u % 2][:], e_th[u % 2][:], 1.0, gu[:, 0:I2], ALU.add, ALU.mult).then_inc(sem("e_t1"), 1)
                dve.wait_ge(sem("e_t1"), pair + 1)
                need(dve, sem("htr"), pair - 1)
                dve.wait_ge(sem(f"gathered{u % 4}"), 16 * (2 * i + u // 4 + 1))
                for e in range(2):
                    q = slice(64 * e, 64 * e + 64)
                    w = g_x[u][q, bass.ds(H + 2 * pair + e, 1)]
                    eh = dve.scalar_tensor_tensor(e_h[u % 2][q, :], e_t1[u % 2][q, :], w, gu[q, I2:2 * I2], ALU.mult, ALU.mult)
                eh.then_inc(sem("e_h"), 1)

            def expert_step(i, u):
                for stage, lag in ((hidden, 2), (equal_slots, 1), (pick, 0)):
                    at = behind(i, u, lag)
                    if at:
                        stage(*at)

            expert_steps(dve, expert_step, 2)


IN_NAMES = ("x", "wq", "wk", "wv", "wo", "gamma", "beta", "wg", "wgu", "wdn", "wsg", "wsu", "wsd", "const")


def kernel(L0_attn_hidden_states, L0_attn_Wq, L0_attn_Wk, L0_attn_Wv, L0_attn_Wo, L0_attn_gamma, L0_attn_beta,
           L0_ffn_gate_w, L0_ffn_gate_up_proj, L0_ffn_down_proj, L0_ffn_shared_gate_w, L0_ffn_shared_up_w,
           L0_ffn_shared_down_w):
    import numpy as _np
    import concourse.bacc as _bacc
    from concourse import mybir as _mybir
    from concourse.bass_utils import run_bass_kernel_spmd as _run

    laid = (L0_attn_hidden_states, L0_attn_Wq.T, L0_attn_Wk.T, L0_attn_Wv.T, L0_attn_Wo.T, L0_attn_gamma, L0_attn_beta,
            L0_ffn_gate_w.T, L0_ffn_gate_up_proj, L0_ffn_down_proj, L0_ffn_shared_gate_w.T, L0_ffn_shared_up_w.T,
            L0_ffn_shared_down_w.T, constants())
    nc = _bacc.Bacc("TRN2", target_bir_lowering=False, num_devices=1)
    arrays, args = {}, []
    for name, a in zip(IN_NAMES, laid):
        a = _np.ascontiguousarray(a)
        arrays[f"in_{name}"] = a
        args.append(nc.dram_tensor(f"in_{name}", a.shape, _mybir.dt.from_np(a.dtype), kind="ExternalInput").ap())
    out = nc.dram_tensor("out_x", (NB, T, H), _mybir.dt.from_np(_np.dtype("float32")), kind="ExternalOutput").ap()
    block_kernel(nc, *args, out)
    got = _run(nc, [arrays], core_ids=[0])
    return got.results[0]["out_x"]
```

```python
from contextlib import ExitStack

import numpy as np
import concourse.bass as bass
from concourse import mybir

F32, F16, BF16 = mybir.dt.float32, mybir.dt.float16, mybir.dt.bfloat16
I32, U32 = mybir.dt.int32, mybir.dt.uint32
ALU = mybir.AluOpType
ACT = mybir.ActivationFunctionType
AX = mybir.AxisListType.X

P = 128
NB, T, H = 16, 256, 256
NT = NB * T
HEADS, D = 16, 16
E, K, CAP = 64, 6, 64
I2 = 96
EPS = 1e-5
PAIRS = E // 2
ROW = H + E
ROWS = NT + P
U = 8

C_ID, C_BLK, C_TRI, C_ONE = 0, 128, 160, 288
C_DIAG, C_IOTA, C_P1, C_DUMP, C_HALF = 416, 424, 432, 433, 441
C_N = 443


def constants():
    c = np.zeros((P, C_N), np.float32)
    p = np.arange(P)
    c[:, C_ID:C_ID + P] = np.eye(P)
    for i in range(8):
        c[16 * i:16 * i + 16, C_BLK + i] = 1.0 / D
    c[:, C_TRI:C_TRI + P] = p[:, None] < p[None, :]
    c[:, C_ONE:C_ONE + P] = 1.0
    c[:, C_DIAG:C_DIAG + 8] = (p[:, None] % 64 // 8) == np.arange(8)
    c[:, C_IOTA:C_IOTA + 8] = np.arange(8)
    c[:, C_P1] = p + 1
    c[:, C_DUMP:C_DUMP + 8] = NT + 1 + (p[:, None] % 16) * 8 + np.arange(8)
    low = p < 64
    c[:, C_HALF] = low
    c[:, C_HALF + 1] = ~low
    return c


class Step:

    def __init__(self, n, parity):
        self.n, self.parity = n, parity

    def batch(self, offset):
        return self.n + offset, (self.parity + offset) % 2


def need(eng, sem, count):
    if isinstance(count, int) and count <= 0:
        return
    eng.wait_ge(sem, count)


def plain_wait(eng, ready, *counts):
    counts = [c for c in counts if not isinstance(c, int)]
    if counts:
        for c in counts:
            eng.to_reg(c)
        eng.wait_ge(ready, 1)


def block_kernel(nc, x, wq, wk, wv, wo, gamma, beta, wg, wgu, wdn, wsg, wsu, wsd, const, out):
    with ExitStack() as ctx:
        def sb(name, shape, dt=F32):
            return ctx.enter_context(nc.sbuf_tensor(name, shape, dt))

        sems = {}

        def sem(name):
            if name not in sems:
                sems[name] = ctx.enter_context(nc.semaphore(name))
            return sems[name]

        def dram(name, shape, dt=F32):
            return nc.dram_tensor(name, shape, dt, kind="Internal").ap()

        q_stack_d = [dram(f"q_stack_d{i}", (HEADS, D, 2, T), F16) for i in range(2)]
        k_stack_d = [dram(f"k_stack_d{i}", (HEADS, D, 2, 2, T), F16) for i in range(2)]
        rows_d = dram("rows_d", (ROWS, ROW))
        table_d = dram("table_d", (E * CAP,))

        bank = [ctx.enter_context(nc.psum_tensor(f"bank{i}", [P, 512], F32)) for i in range(8)]
        S_BANK, O_BANK, G_BANK = bank[0:4], bank[4], bank[5:8]

        cst = sb("cst", [P, C_N])
        ident = cst[:, C_ID:C_ID + P]
        blk = cst[:, C_BLK:C_BLK + 32]
        tri_b = sb("tri_b", [P, P], BF16)
        one_b = sb("one_b", [P, P], BF16)
        x_all = sb("x_all", [P, 2 * NB, H])
        w_raw = sb("w_raw", [P, 2, 768])
        w_tmp = sb("w_tmp", [P, 2, 256])
        w_mean = sb("w_mean", [P, 2, HEADS])
        gb = sb("gb", [P, 2, D])
        b_col = sb("b_col", [P, 1])
        b_mean = sb("b_mean", [P, 1])
        b_c = sb("b_c", [P, 1])
        w_hi = sb("w_hi", [P, 2, 768], F16)
        w_lo = sb("w_lo", [P, 2, 768], F16)
        wo_s = sb("wo_s", [P, 2, H])
        s_raw = sb("s_raw", [P, 2, 448])
        s_hi = sb("s_hi", [P, 2, 448], F16)
        s_lo = sb("s_lo", [P, 2, 448], F16)
        wsd_s = sb("wsd_s", [P, 2, H])
        st1 = sb("st1", [P, 2, 6])
        mv1 = sb("mv1", [P, 2, 2])
        ve1 = sb("ve1", [P, 2])
        rs1 = sb("rs1", [P, 2])
        mhalf = sb("mhalf", [P, 2])
        xn = [sb(f"xn{i}", [P, 2, H]) for i in range(2)]
        x_hi = sb("x_hi", [P, 2, T], F16)
        x_lo = sb("x_lo", [P, 2, T], F16)
        q_hl = [sb(f"q_hl{i}", [P, 2, 2, T], F16) for i in range(2)]
        k_hl = [sb(f"k_hl{i}", [P, 2, 2, T], F16) for i in range(2)]
        q_sq = sb("q_sq", [P, 2, T])
        k_sq = sb("k_sq", [P, 2, T])
        var_t = sb("var_t", [P, T])
        k_rec = sb("k_rec", [P, 2, HEADS])
        qk_var = [sb(f"qk_var{i}", [P, 2, 2, HEADS]) for i in range(2)]
        v_w = [sb(f"v_w{i}", [P, 2, HEADS, 32]) for i in range(2)]
        q_st = [sb(f"q_st{i}", [P, 8, T], F16) for i in range(2)]
        k_st = [sb(f"k_st{i}", [P, 8, T], F16) for i in range(2)]
        a_sq = sb("a_sq", [P, 8, 384])
        o_t = sb("o_t", [P, 4, T])
        den = sb("den", [P, 2, HEADS])
        rec = sb("rec", [P, 2, HEADS])
        o_n = sb("o_n", [P, 2, H])
        o_nt = sb("o_nt", [P, 2, T])
        st2 = sb("st2", [P, 2, 6])
        mv2 = sb("mv2", [P, 2, 2])
        ve2 = sb("ve2", [P, 2])
        rs2 = sb("rs2", [P, 2])
        row = [sb(f"row{i}", [P, 2, ROW]) for i in range(2)]
        x2_hi = sb("x2_hi", [P, 2, T], F16)
        x2_lo = sb("x2_lo", [P, 2, T], F16)
        th = sb("th", [P, T + P])
        t1 = sb("t1", [P, T + P])
        hs = sb("hs", [P, T + P])
        y = [sb(f"y{i}", [P, 2, H]) for i in range(2)]
        gneg = sb("gneg", [P, 2])
        gsum = sb("gsum", [P, 2])
        grec = sb("grec", [P, 2])
        ex = sb("ex", [P, 2, 72])
        top = sb("top", [P, 2, 8])
        top6 = sb("top6", [P, 2, 8])
        marked = sb("marked", [P, 2, 72])
        chosen = [sb(f"chosen{i}", [P, 2, E], BF16) for i in range(2)]
        before = [sb(f"before{i}", [P, E], BF16) for i in range(2)]
        both = sb("both", [P, E], BF16)
        pos_f = sb("pos_f", [P, 2 * E])
        pos_i = sb("pos_i", [P, 2 * E], I32)
        pos_lo = sb("pos_lo", [P, 2 * E], I32)
        pos_hi = sb("pos_hi", [P, 2 * E], I32)
        tile_no = sb("tile_no", [P, 2])
        hi_hot = sb("hi_hot", [P, 2, E, 8], BF16)
        lo_hot = sb("lo_hot", [P, 2, E, 8], BF16)
        tok_hot = sb("tok_hot", [P, 2, E, 2, 8], BF16)
        table = sb("table", [P, 4, 8, 16])
        tab_s = sb("tab_s", [P, 4, 16])
        tab_t = sb("tab_t", [P, 4, 8])
        tab_e = sb("tab_e", [P, 4, 8])
        tab_u = sb("tab_u", [P, 4, 8])
        tab_r = sb("tab_r", [PAIRS, P])
        slot_tok = sb("slot_tok", [P, PAIRS], U32)
        slot_f = sb("slot_f", [P, PAIRS])
        idx_g = sb("idx_g", [P, U], U32)
        idx_s = sb("idx_s", [P, U], U32)
        twice = sb("twice", [P, U])
        picked = [sb(f"picked{i}", [PAIRS, P]) for i in range(2)]
        zero = sb("zero", [P, ROW])
        w_gu = [sb(f"w_gu{i}", [P, 2, 2, 2 * I2]) for i in range(U)]
        w_dn = [sb(f"w_dn{i}", [I2, 2, H]) for i in range(U)]
        spare = x_all[:].rearrange("p s m -> p (s m)")
        g_x = [spare[:, ROW * i:ROW * i + ROW] for i in range(U)]
        e_0 = U * ROW
        g_xt = [spare[:, e_0 + H * i:e_0 + H * i + H].rearrange("p (c s) -> p c s", c=2) for i in range(2)]
        e_o = [spare[:, e_0 + 2 * H + H * i:e_0 + 3 * H + H * i] for i in range(4)]
        same = [spare[:, e_0 + 6 * H + H * i:e_0 + 7 * H + H * i].rearrange("p (e s) -> p e s", e=2) for i in range(4)]
        e_th = [sb(f"e_th{i}", [P, I2]) for i in range(2)]
        e_t1 = [sb(f"e_t1{i}", [P, I2]) for i in range(2)]
        e_h = [sb(f"e_h{i}", [P, I2]) for i in range(2)]
        e_ht = [spare[0:I2, e_0 + 10 * H + H * i:e_0 + 11 * H + H * i].rearrange("p (e s) -> p e s", e=2) for i in range(2)]

        x_d = x.rearrange("b (t p) h -> b p t h", p=P)
        out_t = out.rearrange("b (t p) h -> b p t h", p=P)
        out_rows = out.rearrange("b t h -> (b t) h")
        rows_t = rows_d[0:NT, :].rearrange("(b t p) h -> b p t h", t=2, p=P)

        USES = ["xtr", "pos", "sg", "otr0", "otr1", "su", "q", "k", "gate", "ontr", "var", "wo",
                "vtr", "v", "so0", "so1", "x2tr", "cmp"]
        STAGE = {"xtr": 1, "q": 1, "k": 1, "var": 1, "vtr": 1, "v": 1, "otr0": -1, "otr1": -1, "ontr": -1,
                 "wo": -1, "x2tr": -1, "sg": -2, "su": -2, "gate": -2, "so0": -2, "so1": -2, "pos": -3, "cmp": -3}

        def g_bank(use):
            return G_BANK[USES.index(use) % 3]

        def run(s, *stages):
            for offset, stage, *more in stages:
                if active(s, offset):
                    stage(*s.batch(offset), *more)

        def active(s, offset):
            return not isinstance(s.n, int) or 0 <= s.n + offset < NB

        def bank_free(pe, b, use):
            i = USES.index(use)
            for back in range(1, 7):
                j = i - 3 * back
                prev = USES[j % 18]
                other = b - STAGE[use] + STAGE[prev] - (0 if j >= 0 else 1)
                if isinstance(other, int) and not 0 <= other < NB:
                    continue
                pe.wait_ge(sem(prev + "_read"), other + 1)
                return

        block = ctx.enter_context(nc.Block())

        def pipeline(eng, body, first=-2):
            for n in range(first, 4):
                body(Step(n, n % 2))
            with eng.Fori(2, 6) as i:
                body(Step(2 * i, 0))
                body(Step(2 * i + 1, 1))
            for n in range(12, NB + 3):
                body(Step(n, n % 2))

        def load_expert(sp, pair, u):
            sp.dma_start(w_gu[u][:], wgu[bass.ds(2 * pair, 2)].rearrange("e (c p) m -> p e c m", p=P)).then_inc(sem(f"w_expert{u}"), 16)
            sp.dma_start(w_dn[u][:], wdn[bass.ds(2 * pair, 2)].rearrange("e p h -> p e h")).then_inc(sem(f"w_expert{u}"), 16)

        def behind(i, u, lag):
            i, u = (i, u - lag) if u >= lag else (i - 1, u - lag + U)
            if isinstance(i, int) and not 0 <= i < PAIRS // U:
                return None
            return U * i + u, u, i

        def expert_steps(eng, step, lag):
            for u in range(U):
                step(0, u)
            with eng.Fori(1, PAIRS // U) as i:
                for u in range(U):
                    step(i, u)
            for u in range(lag):
                step(PAIRS // U, u)

        @block.sync
        def _(sp):
            sp.dma_start(x_all[:, 0:2, :], x_d[0]).then_inc(sem("x_in0"), 16)
            for i, w in enumerate((gamma, beta)):
                sp.dma_start(gb[:, i, :], w.rearrange("(o d) -> o d", o=1).to_broadcast([P, D])).then_inc(sem("gb_in"), 16)
            sp.dma_start(b_col[:], beta.rearrange("(o d w) -> o d w", o=1, w=1).to_broadcast([8, D, 1])).then_inc(sem("gb_in"), 16)
            for i, w in enumerate((wq, wk, wv)):
                sp.dma_start(w_raw[:, :, 256 * i:256 * i + 256],
                             w.rearrange("(c p) m -> p c m", p=P)).then_inc(sem(f"w_in{i}"), 16)
                if i == 0:
                    sp.dma_start(cst[:], const).then_inc(sem("const_in"), 16)
            sp.dma_start(x_all[:, 2:4, :], x_d[1]).then_inc(sem("x_in1"), 16)
            sp.dma_start(x_all[:, 4:6, :], x_d[2]).then_inc(sem("x_in"), 16)
            sp.dma_start(wo_s[:], wo.rearrange("(c p) m -> p c m", p=P)).then_inc(sem("s_in"), 16)
            for i, (w, m) in enumerate(((wsg, 192), (wsu, 192), (wg, 64))):
                sp.dma_start(s_raw[:, :, 192 * i:192 * i + m],
                             w.rearrange("(c p) m -> p c m", p=P)).then_inc(sem("s_in"), 16)
            sp.dma_start(wsd_s[:, 0, :], wsd[0:P]).then_inc(sem("s_in"), 16)
            for half in range(2):
                sp.dma_start(wsd_s[64 * half:64 * half + 64, 1, :], wsd[P:P + 64]).then_inc(sem("s_in"), 16)
            sp.wait_ge(sem("zeroed"), 1)
            sp.dma_start(rows_d[NT:ROWS, :], zero[:]).then_inc(sem("zero_out"), 16)

            def body(s):
                if active(s, 3) and not (isinstance(s.n, int) and s.n < 0):
                    b, _p = s.batch(3)
                    sp.wait_ge(sem("x_in"), 16 * (s.n + 1))
                    sp.dma_start(x_all[:, bass.ds(2 * b, 2), :],
                                 x_d[bass.ds(b, 1)].rearrange("o p t h -> p (o t) h")).then_inc(sem("x_in"), 16)
                if active(s, -3):
                    b, p = s.batch(-3)
                    sp.wait_ge(sem("so1_read"), b + 1)
                    sp.dma_start(out_t[bass.ds(b, 1)].rearrange("o p t h -> p (o t) h"), y[p][:]).then_inc(sem("y_out"), 16)
                    sp.wait_ge(sem("row"), b + 1)
                    sp.dma_start(rows_t[bass.ds(b, 1)].rearrange("o p t h -> p (o t) h"), row[p][:]).then_inc(sem("row_out"), 16)
                if active(s, 1):
                    b, p = s.batch(1)
                    plain_wait(sp, sem("ready"), 32 * (b - 1), 16 * (b - 1), b + 1)
                    sp.wait_ge(sem("q_read"), b + 1)
                    need(sp, sem("q_in"), 32 * (b - 1))
                    to = q_stack_d[p].rearrange("(c h) d part t -> (h d) c (part t)", c=2)
                    sp.dma_start(to, q_hl[p][:].rearrange("p c part t -> p c (part t)")).then_inc(sem("q_out"), 16)
                    sp.wait_ge(sem("k_read"), b + 1)
                    need(sp, sem("k_in"), 16 * (b - 1))
                    to = k_stack_d[p].rearrange("(c h) d rep part t -> rep (h d) c (part t)", c=2)
                    for rep in range(2):
                        sp.dma_start(to[rep], k_hl[p][:].rearrange("p c part t -> p c (part t)")).then_inc(sem("k_out"), 16)
                    plain_wait(sp, sem("ready"), 32 * (b + 1), 16 * (b + 1), b - 1)
                    need(sp, sem("score7"), b - 1)
                    sp.wait_ge(sem("q_out"), 16 * (b + 1))
                    back = q_stack_d[p].rearrange("(g hh) d part t -> (hh d part) g t", hh=2)
                    for rep in range(2):
                        sp.dma_start(q_st[p][rep:P:2], back).then_inc(sem("q_in"), 16)
                    sp.wait_ge(sem("k_out"), 32 * (b + 1))
                    back = k_stack_d[p].rearrange("(g hh) d rep part t -> (hh d rep part) g t", hh=2)
                    sp.dma_start(k_st[p][:], back).then_inc(sem("k_in"), 16)

                if isinstance(s.n, int) and s.n >= 12:
                    for i in (s.n - 12, U - 1)[:2 if s.n == 18 else 1]:
                        load_expert(sp, i, i)

            pipeline(sp, body)

            sp.wait_ge(sem("tab_u"), 1)
            sp.dma_start(table_d.rearrange("(g p b) -> p g b", g=4, p=P), tab_u[:]).then_inc(sem("table_out"), 16)
            sp.wait_ge(sem("table_out"), 16)
            sp.dma_start(tab_r[:], table_d.rearrange("(g p) -> g p", p=P)).then_inc(sem("table_in"), 16)
            with sp.Fori(0, PAIRS // U - 1) as i:
                for u in range(U):
                    plain_wait(sp, sem("ready"), U * i + u + 3)
                    need(sp, sem("htr"), U * i + u + 3)
                    load_expert(sp, U * i + U + u, u)
            sp.wait_ge(sem("added"), 16 * PAIRS)

        @block.tensor
        def _(pe):
            def split3(o, w, xx, first, last):
                pe.matmul(o, w[0], xx[0], start=first, stop=False)
                pe.matmul(o, w[1], xx[0], start=False, stop=False)
                return pe.matmul(o, w[0], xx[1], start=False, stop=last)

            def scores(b, p, g):
                if g == 0:
                    pe.wait_ge(sem("q_in"), 32 * (b + 1))
                    pe.wait_ge(sem("k_in"), 16 * (b + 1))
                for h in range(4 * g, 4 * g + 4):
                    if h % 2 == 0:
                        pair = h // 2
                        need(pe, sem(f"square{(pair - 2) % 8}"), b + 1 if pair >= 2 else b)
                    q = 64 * (h % 2)
                    o = S_BANK[h % 4]
                    kk, qq = k_st[p][q:q + 64, h // 2, :], q_st[p][q:q + 64, h // 2, :]
                    pe.matmul(o[:, 0:128], kk[:, 128:256], qq[:, 128:256], start=True, stop=True, tile_position=(q, 0))
                    mm = pe.matmul(o[:, 128:384], kk[:, 0:128], qq, start=True, stop=True, tile_position=(q, 0))
                    if h % 2:
                        mm.then_inc(sem(f"score{h // 2}"), 1)

            def values(b, p, g):
                if g == 0:
                    pe.wait_ge(sem("v_read"), b + 1)
                pe.wait_ge(sem(f"masked{g}"), b + 1)
                if g % 2 == 0:
                    need(pe, sem("o_read1") if g == 0 else sem("o_read0"), b if g == 0 else b + 1)
                c = 256 * (g % 2)
                for j in range(4):
                    h = 4 * g + j
                    pe.matmul(O_BANK[32 * j:32 * j + 32, c:c + 256], v_w[p][:, 0, h, :], a_sq[:, h % 8, 128:384],
                              start=True, stop=False, tile_position=(0, 32 * j), skip_group_check=True)
                for j in range(4):
                    h = 4 * g + j
                    mm = pe.matmul(O_BANK[32 * j:32 * j + 32, c + 128:c + 256], v_w[p][:, 1, h, :], a_sq[:, h % 8, 0:128],
                                   start=False, stop=True, tile_position=(0, 32 * j), skip_group_check=True)
                mm.then_inc(sem(f"value{g}"), 1)

            def transposes(use, src):
                o = g_bank(use)
                for c in range(2):
                    for t in range(2):
                        tr = pe.transpose(o[:, 256 * c + 128 * t:256 * c + 128 * t + 128], src[:, t, 128 * c:128 * c + 128], ident)
                tr.then_inc(sem(use), 1)

            def x_transposes(b, p):
                bank_free(pe, b, "xtr")
                pe.wait_ge(sem("xn"), b + 1)
                transposes("xtr", xn[p])

            def attention_transposes(b, p, t):
                bank_free(pe, b, f"otr{t}")
                pe.wait_ge(sem("o_read1"), b + 1)
                for g in range(4):
                    tr = pe.transpose(g_bank(f"otr{t}")[:, 128 * g:128 * g + 128], o_t[:, g, 128 * t:128 * t + 128], ident)
                tr.then_inc(sem(f"otr{t}"), 1)

            def normalised_transposes(b, p):
                bank_free(pe, b, "ontr")
                pe.wait_ge(sem("otr1_read"), b + 1)
                transposes("ontr", o_n)

            def x2_transposes(b, p):
                bank_free(pe, b, "x2tr")
                pe.wait_ge(sem("x2n"), b + 1)
                transposes("x2tr", row[p])

            def variance_transposes(b, p):
                bank_free(pe, b, "vtr")
                pe.wait_ge(sem("var_read"), b + 1)
                for t in range(2):
                    tr = pe.transpose(g_bank("vtr")[:, 128 * t:128 * t + 128], var_t[:, 128 * t:128 * t + 128], ident)
                tr.then_inc(sem("vtr"), 1)

            def project(b, p, use, first_col):
                bank_free(pe, b, use)
                pe.wait_ge(sem("xtr_read"), b + 1)
                for m in range(2):
                    o = g_bank(use)[:, 256 * m:256 * m + 256]
                    for c in range(2):
                        cols = slice(first_col + 128 * m, first_col + 128 * m + 128)
                        mm = split3(o, (w_hi[:, c, cols], w_lo[:, c, cols]), (x_hi[:, c, :], x_lo[:, c, :]), c == 0, c == 1)
                mm.then_inc(sem(use), 1)

            def project_q(b, p):
                project(b, p, "q", 0)

            def project_k(b, p):
                project(b, p, "k", 256)

            def project_v(b, p):
                bank_free(pe, b, "v")
                for t in range(2):
                    for c in range(2):
                        tok = slice(128 * t, 128 * t + 128)
                        mm = split3(g_bank("v")[:, 256 * t:256 * t + 256], (x_hi[:, c, tok], x_lo[:, c, tok]),
                                    (w_hi[:, c, 512:768], w_lo[:, c, 512:768]), c == 0, c == 1)
                mm.then_inc(sem("v"), 1)

            def variances(b, p):
                bank_free(pe, b, "var")
                pe.wait_ge(sem("q_sq"), b + 1)
                pe.wait_ge(sem("k_sq"), b + 1)
                for j in range(4):
                    mm = pe.matmul(g_bank("var")[32 * j:32 * j + 32, 0:256], blk, (q_sq, k_sq)[j // 2][:, j % 2, :],
                                   start=True, stop=True, tile_position=(0, 32 * j))
                mm.then_inc(sem("var"), 1)

            def output_projection(b, p):
                bank_free(pe, b, "wo")
                pe.wait_ge(sem("ontr_read"), b + 1)
                for t in range(2):
                    for c in range(2):
                        mm = pe.matmul(g_bank("wo")[:, 256 * t:256 * t + 256], o_nt[:, c, 128 * t:128 * t + 128],
                                       wo_s[:, c, :], start=c == 0, stop=c == 1)
                mm.then_inc(sem("wo"), 1)

            def shared_up(b, p, use, first):
                bank_free(pe, b, use)
                pe.wait_ge(sem("x2tr_read"), b + 1)
                for c in range(2):
                    cols = slice(first, first + P)
                    split3(g_bank(use)[:, 0:T], (s_hi[:, c, cols], s_lo[:, c, cols]), (x2_hi[:, c, :], x2_lo[:, c, :]), c == 0, c == 1)
                cols = slice(first + P, first + P + 64)
                for c in range(2):
                    for w, xx in ((s_hi, x2_hi), (s_lo, x2_hi), (s_hi, x2_lo)):
                        for t in range(2):
                            mm = pe.matmul(g_bank(use)[64 * t:64 * t + 64, T:T + P], w[:, c, cols], xx[:, c, 128 * t:128 * t + 128],
                                           start=c == 0 and w is s_hi and xx is x2_hi, stop=c == 1 and xx is x2_lo,
                                           tile_position=(0, 64 * t), skip_group_check=True)
                mm.then_inc(sem(use), 1)

            def shared_down(b, p, t):
                bank_free(pe, b, f"so{t}")
                pe.wait_ge(sem("su_read"), b + 1)
                o, q = g_bank(f"so{t}")[:, 0:H], slice(64 * t, 64 * t + 64)
                pe.matmul(o, hs[:, 128 * t:128 * t + 128], wsd_s[:, 0, :], start=True, stop=False)
                pe.matmul(o, hs[q, T:T + P], wsd_s[q, 1, :], start=False, stop=True, tile_position=(64 * t, 0)).then_inc(sem(f"so{t}"), 1)

            def gate(b, p):
                bank_free(pe, b, "gate")
                for t in range(2):
                    for c in range(2):
                        tok = slice(128 * t, 128 * t + 128)
                        mm = split3(g_bank("gate")[:, 64 * t:64 * t + 64], (x2_hi[:, c, tok], x2_lo[:, c, tok]),
                                    (s_hi[:, c, 384:448], s_lo[:, c, 384:448]), c == 0, c == 1)
                mm.then_inc(sem("gate"), 1)

            def count_before(b, p):
                bank_free(pe, b, "pos")
                pe.wait_ge(sem("chosen"), b + 1)
                pe.wait_ge(sem("before"), b + 1)
                o = g_bank("pos")
                pe.matmul(o[:, 0:64], one_b[:], before[p][:], start=True, stop=False)
                pe.matmul(o[:, 0:64], tri_b[:], chosen[p][:, 0, :], start=False, stop=True)
                pe.matmul(o[:, 64:128], one_b[:], before[p][:], start=True, stop=False)
                pe.matmul(o[:, 64:128], one_b[:], chosen[p][:, 0, :], start=False, stop=False)
                pe.matmul(o[:, 64:128], tri_b[:], chosen[p][:, 1, :], start=False, stop=True).then_inc(sem("pos"), 1)

            def compact(b, p):
                bank_free(pe, b, "cmp")
                pe.wait_ge(sem("tok_hot"), b + 1)
                for gr in range(4):
                    for t in range(2):
                        for half in range(2):
                            ex8 = slice(16 * gr + 8 * half, 16 * gr + 8 * half + 8)
                            mm = pe.matmul(g_bank("cmp")[64 * half:64 * half + 64, 128 * gr:128 * gr + 128],
                                           hi_hot[:, t, ex8, :].rearrange("p e a -> p (e a)"),
                                           tok_hot[:, t, ex8, :, :].rearrange("p e w b -> p (e w b)"),
                                           start=t == 0, stop=t == 1, tile_position=(0, 64 * half), skip_group_check=True)
                mm.then_inc(sem("cmp"), 1)

            ORDER = ((1, x_transposes), (0, scores, 0), (-3, count_before), (-2, shared_up, "sg", 0),
                     (-1, attention_transposes, 0), (0, scores, 1), (-1, attention_transposes, 1),
                     (-2, shared_up, "su", 192), (1, project_q), (1, project_k), (-2, gate), (0, values, 0),
                     (-1, normalised_transposes), (0, values, 1), (0, scores, 2), (1, variances), (-1, output_projection),
                     (1, variance_transposes), (0, scores, 3), (1, project_v), (0, values, 2), (-2, shared_down, 0),
                     (-2, shared_down, 1), (-1, x2_transposes), (0, values, 3), (-3, compact))

            def body(s):
                run(s, *ORDER)

            pe.wait_ge(sem("const_in"), 16)
            run(Step(-1, 1), (1, x_transposes))
            pe.wait_ge(sem("w_ready"), 1)
            run(Step(-1, 1), (1, project_q))
            pe.wait_ge(sem("w_ready"), 2)
            run(Step(-1, 1), (1, project_k))
            run(Step(-1, 1), (1, variances), (1, variance_transposes))
            pe.wait_ge(sem("w_ready"), 3)
            run(Step(-1, 1), (1, project_v))
            body(Step(0, 0))
            pe.wait_ge(sem("s_in"), 16 * 7)
            body(Step(1, 1))
            pe.wait_ge(sem("s_ready"), 1)
            pipeline(pe, body, 2)

            def gather_t(pair, u, i):
                pe.wait_ge(sem(f"gathered{u % 4}"), 16 * (2 * i + u // 4 + 1))
                need(pe, sem("g_xt"), pair - 1)
                o = bank[u % 2]
                for c in range(2):
                    tr = pe.transpose(o[:, 128 * c:128 * c + 128], g_x[u][:, 128 * c:128 * c + 128], ident)
                tr.then_inc(sem("gtr"), 1)

            def tokens(pair, u, i):
                need(pe, sem("same"), pair)
                pe.wait_ge(sem("picked"), pair + 1)
                pe.matmul(bank[7][:, 0:P], cst[0:PAIRS, C_ONE:C_ONE + P], picked[u % 2][:],
                          start=True, stop=True).then_inc(sem("tokens"), 1)

            def gate_up(pair, u, i):
                pe.wait_ge(sem("g_xt"), pair + 1)
                pe.wait_ge(sem(f"w_expert{u}"), 32 * (i + 1))
                need(pe, sem("e_h"), pair - 1)
                o = bank[2 + u % 2]
                for c in range(2):
                    for e in range(2):
                        mm = pe.matmul(o[64 * e:64 * e + 64, 0:2 * I2], g_xt[u % 2][:, c, 64 * e:64 * e + 64], w_gu[u][:, e, c, :],
                                       start=c == 0, stop=c == 1, tile_position=(0, 64 * e), skip_group_check=True)
                mm.then_inc(sem("gu"), 1)

            def hidden_t(pair, u, i):
                pe.wait_ge(sem("e_h"), pair + 1)
                pe.wait_ge(sem("same"), pair + 1)
                need(pe, sem("e_ht"), pair - 1)
                pe.matmul(bank[4 + u % 2][0:I2, 0:2 * P], e_h[u % 2][:], same[u % 4].rearrange("p e s -> p (e s)"),
                          start=True, stop=True).then_inc(sem("htr"), 1)

            def down(pair, u, i):
                pe.wait_ge(sem("e_ht"), pair + 1)
                need(pe, sem("e_o"), pair)
                for e in range(2):
                    mm = pe.matmul(bank[6][:, 0:H], e_ht[u % 2][:, e, :], w_dn[u][:, e, :], start=e == 0, stop=e == 1)
                mm.then_inc(sem("e_down"), 1)

            def expert_step(i, u):
                for stage, lag in ((gather_t, 1), (gate_up, 2), (tokens, 1), (hidden_t, 3), (down, 4)):
                    at = behind(i, u, lag)
                    if at:
                        stage(*at)

            pe.wait_ge(sem("o_read1"), NB)
            pe.wait_ge(sem("cmp_read"), NB)
            pe.wait_ge(sem("pos_read"), NB)
            pe.wait_ge(sem("table_in"), 16)
            pe.transpose(bank[0][:, 0:PAIRS], tab_r[:], ident[0:PAIRS, 0:PAIRS]).then_inc(sem("table_t"), 1)
            pe.wait_ge(sem("slots"), 2)
            expert_steps(pe, expert_step, 4)

        @block.scalar
        def _(act):
            def squares(b, p, pair):
                act.wait_ge(sem(f"score{pair}"), b + 1)
                need(act, sem(f"value{(pair // 2 - 2) % 4}"), b + 1 if pair >= 4 else b)
                for h in (2 * pair, 2 * pair + 1):
                    sq = act.activation(a_sq[:, h % 8, :], S_BANK[h % 4][:, 0:384], ACT.Square)
                sq.then_inc(sem(f"square{pair}"), 1)

            def out_copy(b, p, half):
                act.wait_ge(sem(f"value{2 * half + 1}"), b + 1)
                if half == 0:
                    need(act, sem("otr1"), b)
                act.copy(o_t[:, 2 * half:2 * half + 2, :].rearrange("p g t -> p (g t)"), O_BANK[:]).then_inc(sem(f"o_read{half}"), 1)

            def flat(ap):
                return ap.rearrange("p c t -> p (c t)")

            def x_high(b, p):
                act.wait_ge(sem("xtr"), b + 1)
                need(act, sem("v"), b)
                act.copy(flat(x_hi[:]), g_bank("xtr")[:]).then_inc(sem("x_hi"), 1)

            def high_and_square(b, p, use, hl, sq):
                act.wait_ge(sem(use), b + 1)
                need(act, sem(use + "_out"), (16 if use == "q" else 32) * (b - 1))
                if use == "q":
                    need(act, sem("var"), b)
                act.activation(hl[p][:, :, 0, :], g_bank(use)[:].rearrange("p (c t) -> p c t", c=2), ACT.Identity,
                               bias=b_c[:, 0:1]).then_inc(sem(use + "_hi"), 1)
                act.activation(flat(sq[:]), g_bank(use)[:], ACT.Square, bias=b_c[:, 0:1]).then_inc(sem(use + "_sq"), 1)

            def normalised_copy(b, p):
                act.wait_ge(sem("ontr"), b + 1)
                need(act, sem("wo"), b)
                act.copy(flat(o_nt[:]), g_bank("ontr")[:]).then_inc(sem("ontr_read"), 1)

            def variance_copy(b, p):
                act.wait_ge(sem("var"), b + 1)
                need(act, sem("vtr"), b)
                act.copy(var_t[:], g_bank("var")[:, 0:256]).then_inc(sem("var_read"), 1)

            def x2_high(b, p):
                act.wait_ge(sem("x2tr"), b + 1)
                need(act, sem("gate"), b)
                act.copy(flat(x2_hi[:]), g_bank("x2tr")[:]).then_inc(sem("x2_hi"), 1)

            def shared_tanh(b, p):
                act.wait_ge(sem("sg"), b + 1)
                need(act, sem("sg_read"), b)
                act.activation(th[:], g_bank("sg")[:, 0:T + P], ACT.Tanh, scale=0.5).then_inc(sem("th"), 1)

            def gate_exp(b, p):
                act.wait_ge(sem("gneg"), b + 1)
                need(act, sem("chosen"), b)
                need(act, sem("row"), b)
                for t in range(2):
                    e = act.activation(ex[:, t, 0:64], g_bank("gate")[:, 64 * t:64 * t + 64], ACT.Exp,
                                       bias=gneg[:, t:t + 1], accum_out=gsum[:, t:t + 1])
                e.then_inc(sem("gate_read"), 1)

            ORDER = ((1, x_high), (0, squares, 0), (0, squares, 1), (-2, shared_tanh), (0, squares, 2), (0, squares, 3),
                     (1, high_and_square, "q", q_hl, q_sq), (1, high_and_square, "k", k_hl, k_sq), (-2, gate_exp),
                     (-1, normalised_copy), (0, squares, 4), (0, out_copy, 0), (0, squares, 5), (1, variance_copy),
                     (0, squares, 6), (0, squares, 7), (-1, x2_high), (0, out_copy, 1))

            def body(s):
                run(s, *ORDER)

            act.wait_ge(sem("ready"), 1)
            run(Step(-1, 1), (1, x_high))
            act.wait_ge(sem("bias"), 1)
            run(Step(-1, 1), (1, high_and_square, "q", q_hl, q_sq), (1, high_and_square, "k", k_hl, k_sq), (1, variance_copy))
            pipeline(act, body, 0)

            def gathered_copy(pair, u, i):
                act.wait_ge(sem("gtr"), pair + 1)
                need(act, sem("gu"), pair - 1)
                act.copy(g_xt[u % 2].rearrange("p c s -> p (c s)"), bank[u % 2][:, 0:256]).then_inc(sem("g_xt"), 1)

            def gate_tanh(pair, u, i):
                act.wait_ge(sem("gu"), pair + 1)
                need(act, sem("e_t1"), pair - 1)
                act.activation(e_th[u % 2][:], bank[2 + u % 2][:, 0:I2], ACT.Tanh, scale=0.5).then_inc(sem("e_th"), 1)

            def hidden_copy(pair, u, i):
                act.wait_ge(sem("htr"), pair + 1)
                need(act, sem("e_down"), pair - 1)
                act.copy(e_ht[u % 2].rearrange("p e s -> p (e s)"), bank[4 + u % 2][0:I2, 0:2 * P]).then_inc(sem("e_ht"), 1)

            def output_copy(pair, u, i):
                act.wait_ge(sem("e_down"), pair + 1)
                need(act, sem("added"), 16 * (pair - 3))
                act.copy(e_o[u % 4], bank[6][:, 0:H]).then_inc(sem("e_o"), 1)

            def expert_step(i, u):
                for stage, lag in ((gathered_copy, 1), (gate_tanh, 2), (hidden_copy, 3), (output_copy, 4)):
                    at = behind(i, u, lag)
                    if at:
                        stage(*at)

            expert_steps(act, expert_step, 4)

        @block.gpsimd
        def _(pool):
            pool.memset(mhalf[:], -0.5).then_inc(sem("setup"), 1)
            pool.memset(zero[:], 0.0).then_inc(sem("zeroed"), 1)
            for i in range(2):
                pool.memset(v_w[i][:].rearrange("p t h c -> p (t h c)"), 0.0).then_inc(sem("setup"), 1)
            pool.memset(ex[:].rearrange("p t e -> p (t e)"), -2.0).then_inc(sem("setup"), 1)
            pool.memset(top6[:].rearrange("p t e -> p (t e)"), -2.0).then_inc(sem("setup"), 1)
            pool.memset(before[0][:], 0.0).then_inc(sem("setup"), 1)
            pool.memset(table[:].rearrange("p g e w -> p (g e w)"), 0.0).then_inc(sem("setup"), 1)
            pool.memset(tile_no[:, 0:1], -2.0).then_inc(sem("setup"), 1)
            pool.memset(tile_no[:, 1:2], -1.0).then_inc(sem("setup"), 1)
            pool.memset(both[:], 0.0).then_inc(sem("setup"), 1)
            pool.wait_ge(sem("setup"), 10)
            pool.memset(w_mean[:], 0.0).then_inc(sem("ready"), 1)

            def masks(b, p, pair):
                plain_wait(pool, sem("ready"), b + 1)
                need(pool, sem(f"square{pair}"), b + 1)
                h = 2 * pair % 8
                a = a_sq[:, h:h + 2, 0:2 * P]
                m = pool.affine_select(out=a, in_=a, pattern=[[0, 2], [0, 2], [1, P]], compare_op=ALU.is_ge, fill=0.0,
                                       base=0, channel_multiplier=-1)
                if pair % 2:
                    m.then_inc(sem(f"masked{pair // 2}"), 1)

            def rsqrt1(b, p):
                pool.wait_ge(sem("ve1"), b + 1)
                need(pool, sem("xn"), b)
                pool.tensor_tensor(rs1[:], ve1[:], mhalf[:], ALU.pow).then_inc(sem("rs1"), 1)

            def rsqrt2(b, p):
                pool.wait_ge(sem("ve2"), b + 1)
                need(pool, sem("x2n"), b)
                pool.tensor_tensor(rs2[:], ve2[:], mhalf[:], ALU.pow).then_inc(sem("rs2"), 1)

            ORDER = ((0, masks, 0), (2, rsqrt1), (0, masks, 1), (0, masks, 2), (0, masks, 3), (0, masks, 4), (0, masks, 5),
                     (0, masks, 6), (0, masks, 7), (-1, rsqrt2))

            def body(s):
                run(s, *ORDER)

            pool.wait_ge(sem("ready"), 1)
            pipeline(pool, body)

            pool.wait_ge(sem("slots"), 2)
            pool.wait_ge(sem("row_out"), 16 * NB)
            pool.wait_ge(sem("y_out"), 16 * NB)
            pool.wait_ge(sem("zero_out"), 16)

            AHEAD = 6

            def gather(pair, u, i):
                need(pool, sem("e_h"), pair - U + 1)
                need(pool, sem(f"gathered{u % 4}"), 16 * (2 * i + u // 4))
                pool.tensor_copy(idx_g[:, u:u + 1], slot_tok[:, bass.ds(pair, 1)]).then_inc(sem("idx"), 1)
                plain_wait(pool, sem("ready"), pair + 1)
                pool.wait_ge(sem("idx"), pair + 1)
                pool.indirect_dma_start(out=g_x[u], out_offset=None, in_=rows_d[:, :],
                                        in_offset=bass.IndirectOffsetOnAxis(ap=idx_g[:, u:u + 1], axis=0)).then_inc(sem(f"gathered{u % 4}"), 16)

            def scatter(pair, u, i):
                plain_wait(pool, sem("ready"), pair + 1, 16 * pair)
                pool.wait_ge(sem("idx_s"), pair + 1)
                pool.wait_ge(sem("e_o"), pair + 1)
                need(pool, sem("added"), 16 * pair)
                pool.indirect_dma_start(out=out_rows, out_offset=bass.IndirectOffsetOnAxis(ap=idx_s[:, u:u + 1], axis=0),
                                        in_=e_o[u % 4], in_offset=None, compute_op=ALU.add,
                                        bounds_check=NT - 1, oob_is_err=False).then_inc(sem("added"), 16)

            def expert_step(i, u):
                at = behind(i, u, AHEAD)
                if at:
                    scatter(*at)
                at = behind(i, u, 0)
                if at:
                    gather(*at)

            expert_steps(pool, expert_step, AHEAD)

        @block.vector
        def _(dve):
            done = [0]

            def chain(ins):
                done[0] += 1
                ins.then_inc(sem("chain"), 1)
                dve.wait_ge(sem("chain"), done[0])

            def flat(ap):
                return ap.rearrange("p c t -> p (c t)")

            def x_of(b):
                return x_all[:, 2 * b:2 * b + 2, :] if isinstance(b, int) else x_all[:, bass.ds(2 * b, 2), :]

            def moments1(b, p):
                if isinstance(b, int) and b < 2:
                    dve.wait_ge(sem(f"x_in{b}"), 16)
                else:
                    plain_wait(dve, sem("ready"), 16 * (b - 1), b + 1)
                    dve.wait_ge(sem("x_in"), 16 * (b - 1))
                for t in range(2):
                    st = dve.bn_stats(st1[:, t, :], x_of(b)[:, t, :])
                st.then_inc(sem("st1"), 1)

            def variance1(b, p):
                plain_wait(dve, sem("ready"), b + 1)
                need(dve, sem("st1"), b + 1)
                for t in range(2):
                    ag = dve.bn_aggr(mv1[:, t, :], st1[:, t, :])
                ag.then_inc(sem("mv1"), 1)

            def eps1(b, p):
                dve.wait_ge(sem("mv1"), b + 1)
                need(dve, sem("rs1"), b)
                dve.tensor_scalar(ve1[:], mv1[:, :, 1], EPS, None, ALU.add).then_inc(sem("ve1"), 1)

            def normalise1(b, p):
                dve.wait_ge(sem("rs1"), b + 1)
                need(dve, sem("xtr"), b - 1)
                for t in range(2):
                    n = dve.tensor_scalar(xn[p][:, t, :], x_of(b)[:, t, :], mv1[:, t, 0:1], rs1[:, t:t + 1], ALU.subtract, ALU.mult)
                n.then_inc(sem("xn"), 1)

            def x_low(b, p):
                dve.wait_ge(sem("x_hi"), b + 1)
                need(dve, sem("v"), b)
                dve.tensor_tensor(flat(x_lo[:]), g_bank("xtr")[:], flat(x_hi[:]), ALU.subtract).then_inc(sem("xtr_read"), 1)

            def low(b, p, use, hl):
                dve.wait_ge(sem(use + "_hi"), b + 1)
                dve.wait_ge(sem(use + "_sq"), b + 1)
                dve.scalar_tensor_tensor(hl[p][:, :, 1, :], g_bank(use)[:].rearrange("p (c t) -> p c t", c=2), b_c[:, 0:1],
                                         hl[p][:, :, 0, :], ALU.add, ALU.subtract).then_inc(sem(use + "_read"), 1)

            def norms(b, p):
                dve.wait_ge(sem("vtr"), b + 1)
                g = g_bank("vtr")[:, 0:256].rearrange("p (t w m i) -> p t w m i", t=2, w=2, m=2)
                for t in range(2):
                    vr = dve.tensor_scalar(qk_var[p][:, t, :, :].rearrange("p w (m i) -> p w m i", m=2), g[:, t, :, :, 0:8], EPS, None, ALU.add)
                vr.then_inc(sem("vtr_read"), 1)

            def invert_norms(b, p):
                dve.wait_ge(sem("vtr_read"), b + 1)
                dve.reciprocal(k_rec[:], qk_var[p][:, :, 1, :]).then_inc(sem("k_rec"), 1)

            def weigh_v(b, p):
                dve.wait_ge(sem("k_rec"), b + 1)
                need(dve, sem("value3"), b - 1)
                dve.wait_ge(sem("v"), b + 1)
                dve.tensor_copy(v_w[p][:, :, :, 16], k_rec[:])
                for t in range(2):
                    r = k_rec[:, t, :].unsqueeze(2).to_broadcast([P, HEADS, D])
                    vv = dve.tensor_tensor(v_w[p][:, t, :, 0:16], g_bank("v")[:, 256 * t:256 * t + 256].rearrange("p (h d) -> p h d", d=D), r, ALU.mult)
                vv.then_inc(sem("v_read"), 1)

            def denominators(b, p):
                for t in range(2):
                    dve.wait_ge(sem(f"otr{t}"), b + 1)
                    o = g_bank(f"otr{t}")[:].rearrange("p (h c) -> p h c", c=32)
                    dd = dve.scalar_tensor_tensor(den[:, t, :], qk_var[p][:, t, 0, :], 16 * EPS, o[:, :, 16], ALU.mult, ALU.add)
                dd.then_inc(sem("den"), 1)

            def invert_denominators(b, p):
                dve.wait_ge(sem("den"), b + 1)
                dve.reciprocal(rec[:].rearrange("p t h -> p (t h)"), den[:].rearrange("p t h -> p (t h)")).then_inc(sem("rec"), 1)

            def divide(b, p):
                dve.wait_ge(sem("rec"), b + 1)
                need(dve, sem("ontr"), b)
                for t in range(2):
                    o = g_bank(f"otr{t}")[:].rearrange("p (h c) -> p h c", c=32)
                    r = rec[:, t, :].unsqueeze(2).to_broadcast([P, HEADS, D])
                    on = dve.tensor_tensor(o_n[:, t, :].rearrange("p (h d) -> p h d", d=D), o[:, :, 0:16], r, ALU.mult)
                    on.then_inc(sem(f"otr{t}_read"), 1)

            def residual(b, p):
                dve.wait_ge(sem("wo"), b + 1)
                xx = x_of(b)
                dve.tensor_tensor(xx, xx, g_bank("wo")[:].rearrange("p (t h) -> p t h", t=2), ALU.add).then_inc(sem("wo_read"), 1)

            def moments2(b, p):
                plain_wait(dve, sem("ready"), b + 1)
                need(dve, sem("wo_read"), b + 1)
                for t in range(2):
                    st = dve.bn_stats(st2[:, t, :], x_of(b)[:, t, :])
                st.then_inc(sem("st2"), 1)

            def variance2(b, p):
                plain_wait(dve, sem("ready"), b + 1)
                need(dve, sem("st2"), b + 1)
                for t in range(2):
                    ag = dve.bn_aggr(mv2[:, t, :], st2[:, t, :])
                ag.then_inc(sem("mv2"), 1)

            def eps2(b, p):
                dve.wait_ge(sem("mv2"), b + 1)
                dve.tensor_scalar(ve2[:], mv2[:, :, 1], EPS, None, ALU.add).then_inc(sem("ve2"), 1)

            def normalise2(b, p):
                dve.wait_ge(sem("rs2"), b + 1)
                need(dve, sem("row_out"), 16 * (b - 1))
                for t in range(2):
                    n = dve.tensor_scalar(row[p][:, t, 0:H], x_of(b)[:, t, :], mv2[:, t, 0:1], rs2[:, t:t + 1], ALU.subtract, ALU.mult)
                n.then_inc(sem("x2n"), 1)

            def x2_low(b, p):
                dve.wait_ge(sem("x2_hi"), b + 1)
                dve.tensor_tensor(flat(x2_lo[:]), g_bank("x2tr")[:], flat(x2_hi[:]), ALU.subtract).then_inc(sem("x2tr_read"), 1)

            def gated(b, p):
                dve.wait_ge(sem("th"), b + 1)
                dve.scalar_tensor_tensor(t1[:], th[:], 1.0, g_bank("sg")[:, 0:T + P], ALU.add, ALU.mult).then_inc(sem("sg_read"), 1)

            def hidden_shared(b, p):
                dve.wait_ge(sem("sg_read"), b + 1)
                dve.wait_ge(sem("su"), b + 1)
                need(dve, sem("so1"), b)
                dve.scalar_tensor_tensor(hs[:], t1[:], 0.5, g_bank("su")[:, 0:T + P], ALU.mult, ALU.mult).then_inc(sem("su_read"), 1)

            def negative_max(b, p):
                dve.wait_ge(sem("gate"), b + 1)
                dve.tensor_reduce(gneg[:], g_bank("gate")[:, 0:128].rearrange("p (t e) -> p t e", t=2), AX, ALU.max,
                                  negate=True).then_inc(sem("gneg"), 1)

            def softmax_sum(b, p):
                dve.wait_ge(sem("gate_read"), b + 1)
                dve.reciprocal(grec[:], gsum[:]).then_inc(sem("grec"), 1)

            def top8(b, p):
                plain_wait(dve, sem("ready"), b + 1)
                need(dve, sem("gate_read"), b + 1)
                for t in range(2):
                    mx = dve.max(top[:, t, :], ex[:, t, 0:64])
                mx.then_inc(sem("top"), 1)

            def weights(b, p):
                dve.wait_ge(sem("grec"), b + 1)
                for t in range(2):
                    gw = dve.tensor_scalar(row[p][:, t, H:ROW], ex[:, t, 0:64], grec[:, t:t + 1], 0.5, ALU.mult, ALU.mult)
                gw.then_inc(sem("row"), 1)

            def keep6(b, p):
                dve.wait_ge(sem("top"), b + 1)
                dve.tensor_copy(top6[:, :, 0:6], top[:, :, 0:6]).then_inc(sem("top6"), 1)

            def mark_chosen(b, p):
                plain_wait(dve, sem("ready"), b + 1)
                need(dve, sem("top6"), b + 1)
                for t in range(2):
                    mr = dve.match_replace(marked[:, t, 0:66], top6[:, t, :], ex[:, t, 0:66], -1.0)
                mr.then_inc(sem("marked"), 1)

            def choice(b, p):
                dve.wait_ge(sem("marked"), b + 1)
                need(dve, sem("pos"), b - 1)
                dve.tensor_scalar(chosen[p][:], marked[:, :, 0:64], 0.0, None, ALU.is_lt).then_inc(sem("chosen"), 1)

            def add_shared(b, p, t):
                if t == 0:
                    need(dve, sem("y_out"), 16 * (b - 1))
                dve.wait_ge(sem(f"so{t}"), b + 1)
                dve.tensor_tensor(y[p][:, t, :], x_of(b)[:, t, :], g_bank(f"so{t}")[:, 0:H], ALU.add).then_inc(sem(f"so{t}_read"), 1)

            def positions(b, p):
                need(dve, sem("tok_hot"), b)
                dve.tensor_scalar(tile_no[:], tile_no[:], 2.0, None, ALU.add).then_inc(sem("tile_no"), 1)
                ch = chosen[p][:].rearrange("p t e -> p (t e)")
                dve.wait_ge(sem("pos"), b + 1)
                dve.scalar_tensor_tensor(pos_f[:], ch, -1024.0, g_bank("pos")[:, 0:128], ALU.mult, ALU.add).then_inc(sem("pos_read"), 1)
                dve.tensor_tensor(both[:], chosen[p][:, 0, :], chosen[p][:, 1, :], ALU.add).then_inc(sem("both"), 1)

            def add_before(b, p):
                dve.wait_ge(sem("both"), b + 1)
                dve.tensor_tensor(before[1 - p][:], before[p][:], both[:], ALU.add).then_inc(sem("before"), 1)

            def slots(b, p):
                dve.wait_ge(sem("pos_read"), b + 1)
                dve.tensor_scalar(pos_i[:], pos_f[:], 1024.0, None, ALU.add).then_inc(sem("pos_i"), 1)

            def digits(b, p):
                dve.wait_ge(sem("pos_i"), b + 1)
                dve.tensor_scalar(pos_lo[:], pos_i[:], 7, None, ALU.bitwise_and)
                dve.tensor_scalar(pos_hi[:], pos_i[:], 3, None, ALU.arith_shift_right).then_inc(sem("digits"), 1)

            def one_hots(b, p):
                dve.wait_ge(sem("digits"), b + 1)
                need(dve, sem("cmp"), b)
                numbers = cst[:, C_IOTA:C_IOTA + 8].unsqueeze(1).to_broadcast([P, 2 * E, 8])
                for dst, src in ((hi_hot, pos_hi), (lo_hot, pos_lo)):
                    hot = dve.tensor_tensor(dst[:].rearrange("p t e d -> p (t e) d"), src[:].unsqueeze(2).to_broadcast([P, 2 * E, 8]),
                                            numbers, ALU.is_equal)
                hot.then_inc(sem("lo_hot"), 1)

            def token_hots(b, p):
                dve.wait_ge(sem("lo_hot"), b + 1)
                dve.wait_ge(sem("tile_no"), b + 1)
                dve.tensor_scalar(tok_hot[:, :, :, 0, :].rearrange("p t e d -> p (t e) d"),
                                  lo_hot[:].rearrange("p t e d -> p (t e) d"), cst[:, C_P1:C_P1 + 1], None, ALU.mult)
                for t in range(2):
                    hot = dve.tensor_scalar(tok_hot[:, t, :, 1, :], lo_hot[:, t, :, :], tile_no[:, t:t + 1], None, ALU.mult)
                hot.then_inc(sem("tok_hot"), 1)

            def add_table(b, p):
                dve.wait_ge(sem("cmp"), b + 1)
                tb = table[:].rearrange("p g e w -> p (g e w)")
                dve.tensor_tensor(tb, tb, g_bank("cmp")[:], ALU.add).then_inc(sem("cmp_read"), 1)

            ORDER = ((1, x_low), (2, moments1), (-3, positions), (2, variance1), (-2, gated), (-1, denominators),
                     (2, eps1), (-3, slots), (-1, invert_denominators), (-1, divide), (-2, hidden_shared), (2, normalise1),
                     (1, low, "q", q_hl), (-3, add_before), (-2, negative_max), (-3, digits), (1, low, "k", k_hl),
                     (-2, softmax_sum), (-3, one_hots), (-3, token_hots), (-2, weights), (-2, top8), (-1, residual),
                     (1, norms), (-1, moments2), (-1, variance2), (-2, keep6), (1, invert_norms), (-1, eps2), (1, weigh_v),
                     (-1, normalise2), (-2, add_shared, 0), (-2, add_shared, 1), (-2, mark_chosen), (-2, choice),
                     (-1, x2_low), (-3, add_table))

            def body(s):
                run(s, *ORDER)

            def heads(a):
                return a.rearrange("p c (h d) -> p c h d", d=D)

            def centre(i):
                w, g, m = w_raw[:, :, 256 * i:256 * i + 256], w_tmp[:], w_mean[:]
                for c in range(2):
                    last = dve.tensor_tensor(heads(g)[:, c], heads(w)[:, c], gb[:, 0:1, :].to_broadcast([P, HEADS, D]), ALU.mult)
                chain(last)
                chain(dve.tensor_reduce(m, heads(g), AX, ALU.add))
                m2 = m.rearrange("p c h -> p (c h)")
                chain(dve.tensor_scalar(m2, m2, 1.0 / D, None, ALU.mult))
                chain(dve.tensor_tensor(heads(w), heads(g), m.unsqueeze(3).to_broadcast([P, 2, HEADS, D]), ALU.subtract))

            def split(i):
                cols = slice(256 * i, 256 * i + 256)
                chain(dve.tensor_copy(w_hi[:, :, cols], w_raw[:, :, cols]))
                dve.tensor_tensor(w_lo[:, :, cols], w_raw[:, :, cols], w_hi[:, :, cols], ALU.subtract).then_inc(sem("w_ready"), 1)

            body(Step(-2, 0))
            dve.wait_ge(sem("ready"), 1)
            dve.wait_ge(sem("gb_in"), 16 * 3)
            dve.wait_ge(sem("w_in0"), 16)
            centre(0)
            split(0)
            run(Step(-1, 1), (1, x_low))
            chain(dve.tensor_reduce(b_mean[:], gb[:, 1, :], AX, ALU.add))
            chain(dve.tensor_scalar(b_mean[:], b_mean[:], 1.0 / D, None, ALU.mult))
            dve.tensor_scalar(b_c[:], b_col[:], b_mean[:, 0:1], None, ALU.subtract).then_inc(sem("bias"), 1)
            dve.wait_ge(sem("w_in1"), 16)
            centre(1)
            split(1)
            dve.wait_ge(sem("bias"), 1)
            run(Step(-1, 1), (1, low, "q", q_hl), (2, moments1), (2, variance1), (2, eps1), (2, normalise1), (1, low, "k", k_hl))
            dve.wait_ge(sem("w_in2"), 16)
            split(2)
            run(Step(-1, 1), (1, norms), (1, invert_norms), (1, weigh_v))
            body(Step(0, 0))
            dve.wait_ge(sem("const_in"), 16)
            dve.wait_ge(sem("s_in"), 16 * 7)
            chain(dve.tensor_copy(flat(s_hi[:]), flat(s_raw[:])))
            dve.tensor_tensor(flat(s_lo[:]), flat(s_raw[:]), flat(s_hi[:]), ALU.subtract).then_inc(sem("s_ready"), 1)
            chain(dve.tensor_copy(tri_b[:], cst[:, C_TRI:C_TRI + P]))
            dve.tensor_copy(one_b[:], cst[:, C_ONE:C_ONE + P]).then_inc(sem("before"), 1)
            pipeline(dve, body, 1)

            dve.wait_ge(sem("cmp_read"), NB)
            diag = cst[:, C_DIAG:C_DIAG + 8].unsqueeze(1).unsqueeze(3).to_broadcast([P, 4, 8, 16])
            chain(dve.tensor_tensor(table[:], table[:], diag, ALU.mult))
            chain(dve.tensor_reduce(tab_s[:], table[:].rearrange("p g e w -> p g w e"), AX, ALU.add))
            place, tile = tab_s[:, :, 0:8], tab_s[:, :, 8:16]
            chain(dve.scalar_tensor_tensor(tab_t[:], tile, float(P), place, ALU.mult, ALU.add))
            dump = cst[:, C_DUMP:C_DUMP + 8].unsqueeze(1).to_broadcast([P, 4, 8])
            chain(dve.scalar_tensor_tensor(tab_e[:], place, 0.0, dump, ALU.is_equal, ALU.mult))
            chain(dve.tensor_tensor(tab_t[:], tab_t[:], tab_e[:], ALU.add))
            dve.tensor_scalar(tab_u[:], tab_t[:], -1.0, None, ALU.add).then_inc(sem("tab_u"), 1)
            dve.wait_ge(sem("table_t"), 1)
            dve.tensor_copy(slot_tok[:], bank[0][:, 0:PAIRS]).then_inc(sem("slots"), 1)
            dve.tensor_copy(slot_f[:], bank[0][:, 0:PAIRS]).then_inc(sem("slots"), 1)
            dve.wait_ge(sem("slots"), 2)

            def pick(pair, u, i):
                need(dve, sem("tokens"), pair - 1)
                dve.tensor_scalar(picked[u % 2][:], tab_r[:], ident[0:PAIRS, bass.ds(pair, 1)], None, ALU.mult).then_inc(sem("picked"), 1)

            def equal_slots(pair, u, i):
                dve.wait_ge(sem("tokens"), pair + 1)
                need(dve, sem("htr"), pair - 3)
                for e in range(2):
                    half = cst[:, C_HALF + e:C_HALF + e + 1]
                    eq = dve.tensor_scalar(same[u % 4][:, e, :], bank[7][:, 0:P], slot_f[:, bass.ds(pair, 1)], half,
                                           ALU.is_equal, ALU.mult)
                eq.then_inc(sem("same"), 1)
                dve.wait_ge(sem("same"), pair + 1)
                dve.tensor_reduce(twice[:, u:u + 1], same[u % 4][:, 1, 0:64], AX, ALU.max).then_inc(sem("twice"), 1)
                dve.wait_ge(sem("twice"), pair + 1)
                need(dve, sem("added"), 16 * (pair - U + 1))
                dve.scalar_tensor_tensor(idx_s[:, u:u + 1], twice[:, u:u + 1], float(2 * NT), slot_f[:, bass.ds(pair, 1)],
                                         ALU.mult, ALU.add).then_inc(sem("idx_s"), 1)

            def hidden(pair, u, i):
                dve.wait_ge(sem("e_th"), pair + 1)
                gu = bank[2 + u % 2]
                dve.scalar_tensor_tensor(e_t1[u % 2][:], e_th[u % 2][:], 1.0, gu[:, 0:I2], ALU.add, ALU.mult).then_inc(sem("e_t1"), 1)
                dve.wait_ge(sem("e_t1"), pair + 1)
                need(dve, sem("htr"), pair - 1)
                dve.wait_ge(sem(f"gathered{u % 4}"), 16 * (2 * i + u // 4 + 1))
                for e in range(2):
                    q = slice(64 * e, 64 * e + 64)
                    w = g_x[u][q, bass.ds(H + 2 * pair + e, 1)]
                    eh = dve.scalar_tensor_tensor(e_h[u % 2][q, :], e_t1[u % 2][q, :], w, gu[q, I2:2 * I2], ALU.mult, ALU.mult)
                eh.then_inc(sem("e_h"), 1)

            def expert_step(i, u):
                for stage, lag in ((hidden, 2), (equal_slots, 1), (pick, 0)):
                    at = behind(i, u, lag)
                    if at:
                        stage(*at)

            expert_steps(dve, expert_step, 2)


IN_NAMES = ("x", "wq", "wk", "wv", "wo", "gamma", "beta", "wg", "wgu", "wdn", "wsg", "wsu", "wsd", "const")


def kernel(L0_attn_hidden_states, L0_attn_Wq, L0_attn_Wk, L0_attn_Wv, L0_attn_Wo, L0_attn_gamma, L0_attn_beta,
           L0_ffn_gate_w, L0_ffn_gate_up_proj, L0_ffn_down_proj, L0_ffn_shared_gate_w, L0_ffn_shared_up_w,
           L0_ffn_shared_down_w):
    import numpy as _np
    import concourse.bacc as _bacc
    from concourse import mybir as _mybir
    from concourse.bass_utils import run_bass_kernel_spmd as _run

    laid = (L0_attn_hidden_states, L0_attn_Wq.T, L0_attn_Wk.T, L0_attn_Wv.T, L0_attn_Wo.T, L0_attn_gamma, L0_attn_beta,
            L0_ffn_gate_w.T, L0_ffn_gate_up_proj, L0_ffn_down_proj, L0_ffn_shared_gate_w.T, L0_ffn_shared_up_w.T,
            L0_ffn_shared_down_w.T, constants())
    nc = _bacc.Bacc("TRN2", target_bir_lowering=False, num_devices=1)
    arrays, args = {}, []
    for name, a in zip(IN_NAMES, laid):
        a = _np.ascontiguousarray(a)
        arrays[f"in_{name}"] = a
        args.append(nc.dram_tensor(f"in_{name}", a.shape, _mybir.dt.from_np(a.dtype), kind="ExternalInput").ap())
    out = nc.dram_tensor("out_x", (NB, T, H), _mybir.dt.from_np(_np.dtype("float32")), kind="ExternalOutput").ap()
    block_kernel(nc, *args, out)
    got = _run(nc, [arrays], core_ids=[0])
    return got.results[0]["out_x"]
```
